# Optimizing a Trainium2 kernel written in Bass

```python
import numpy as np
import jax
import jax.numpy as jnp

def _softmax(x, axis=-1):
    return jax.nn.softmax(x, axis=axis)

def _gelu(x):
    return jax.nn.gelu(x, approximate=True)

def _silu(x):
    return jax.nn.silu(x)

def _sigmoid(x):
    return jax.nn.sigmoid(x)

def _layernorm(x, axis=-1, eps=1e-05):
    m = jnp.mean(x, axis=axis, keepdims=True)
    v = jnp.var(x, axis=axis, keepdims=True)
    return (x - m) / jnp.sqrt(v + eps)

def _scatter_add(tgt, idx, src, axis=0):
    return tgt.at[idx].add(src)

def _segment_sum(src, seg, n):
    return jax.ops.segment_sum(src, seg, n)
kernel_name = 'mk_prb_d2_jaxref_r8_9d6a14'

def setup_inputs(seed: int=0):
    np.random.seed(seed)
    _w = jnp.asarray

    def _L0_attn_setup():
        import jax, jax.numpy as jnp
        import numpy as np
        import math
        D_MODEL = 128
        N_HEADS = 16
        D_K = D_MODEL // N_HEADS
        BATCH = 4
        SEQ = 256
        TRAINING_PROGRESS = 0.25
        CONVERGENCE_PHASE = 0.5
        TENSION = abs(1.0 - 1.0)

        def _pos_encoding(seq_len, d, yellow):
            phase_mod = 0.1 * math.sin(2.0 * math.pi * TRAINING_PROGRESS)
            i_even = jnp.arange(0, d, 2, dtype=jnp.float32)
            denom = jnp.power(10000.0, 2.0 * i_even / d) * (1.0 + yellow * phase_mod)
            pos = jnp.arange(seq_len, dtype=jnp.float32)
            ang = pos[:, None] / denom[None, :]
            pe = jnp.zeros((seq_len, d), jnp.float32)
            pe = pe.at[:, 0::2].set(jnp.sin(ang))
            pe = pe.at[:, 1::2].set(jnp.cos(ang))
            return pe
        key = jax.random.key(seed)
        ks = jax.random.split(key, 8)
        x = jax.random.normal(ks[0], (BATCH, SEQ, D_MODEL), dtype=jnp.float32)
        rby = jax.random.uniform(ks[1], (3,), dtype=jnp.float32)
        s = 0.02
        Wq = jax.random.normal(ks[2], (D_MODEL, D_MODEL), dtype=jnp.float32) * s
        Wk = jax.random.normal(ks[3], (D_MODEL, D_MODEL), dtype=jnp.float32) * s
        Wv = jax.random.normal(ks[4], (D_MODEL, D_MODEL), dtype=jnp.float32) * s
        Wo = jax.random.normal(ks[5], (D_MODEL, D_MODEL), dtype=jnp.float32) * s
        bq = jnp.zeros((D_MODEL,), jnp.float32)
        bk = jnp.zeros((D_MODEL,), jnp.float32)
        bv = jnp.zeros((D_MODEL,), jnp.float32)
        bo = jnp.zeros((D_MODEL,), jnp.float32)
        ln_gamma = jnp.ones((D_MODEL,), jnp.float32)
        ln_beta = jnp.zeros((D_MODEL,), jnp.float32)
        return {'x': x, 'rby': rby, 'Wq': Wq, 'bq': bq, 'Wk': Wk, 'bk': bk, 'Wv': Wv, 'bv': bv, 'Wo': Wo, 'bo': bo, 'ln_gamma': ln_gamma, 'ln_beta': ln_beta}
    _L0_attn_in = _L0_attn_setup()

    def _L0_ffn_setup():
        import jax, jax.numpy as jnp
        import numpy as np
        key = jax.random.key(seed)
        k0, k1, k2, k3 = jax.random.split(key, 4)
        B, S, D, F, E = (8, 256, 128, 256, 8)
        x = jax.random.normal(k0, (B, S, D), dtype=jnp.float32)
        Wg = jax.random.normal(k1, (D, E), dtype=jnp.float32) * 0.02
        W1 = jax.random.normal(k2, (E, D, F), dtype=jnp.float32) * 0.02
        W2 = jax.random.normal(k3, (E, F, D), dtype=jnp.float32) * 0.02
        return {'x': x, 'Wg': Wg, 'W1': W1, 'W2': W2}
    _L0_ffn_in = _L0_ffn_setup()

    def _L1_attn_setup():
        import math
        import jax, jax.numpy as jnp
        import numpy as np
        B, N, D = (4, 512, 128)
        H, M = (16, 64)
        HD = D // H
        EPS = 1e-06

        def favor_features(data, proj):
            hd = data.shape[-1]
            m = proj.shape[0]
            dn = data / math.sqrt(hd)
            norm_sq = 0.5 * jnp.sum(dn * dn, axis=-1, keepdims=True)
            comb = jnp.einsum('bhnd,md->bhnm', dn, proj) - norm_sq
            comb = comb - jnp.max(comb, axis=-1, keepdims=True)
            return jnp.exp(comb) / math.sqrt(m) + EPS
        key = jax.random.key(seed)
        ks = jax.random.split(key, 6)
        x = jax.random.normal(ks[0], (B, N, D), dtype=jnp.float32)
        qkv_w = jax.random.normal(ks[1], (3 * D, D), dtype=jnp.float32) * (1.0 / math.sqrt(D))
        qkv_b = jnp.zeros((3 * D,), dtype=jnp.float32)
        proj_w = jax.random.normal(ks[2], (D, D), dtype=jnp.float32) * (1.0 / math.sqrt(D))
        proj_b = jnp.zeros((D,), dtype=jnp.float32)
        pm = jax.random.normal(ks[3], (M, HD), dtype=jnp.float32)
        pm = pm / jnp.linalg.norm(pm, axis=-1, keepdims=True)
        return {'x': x, 'qkv_w': qkv_w, 'qkv_b': qkv_b, 'proj_w': proj_w, 'proj_b': proj_b, 'projection_matrix': pm}
    _L1_attn_in = _L1_attn_setup()

    def _L1_ffn_setup():
        import jax, jax.numpy as jnp
        import numpy as np
        H, I, E, NS, C = (128, 128, 6, 2, 2)
        TOPK = 2
        TEMP = 1.0
        EPS = 1e-06
        key = jax.random.key(seed)
        ks = jax.random.split(key, 20)
        sd = 0.02
        inp = {'x': jax.random.normal(ks[0], (4, 256, H), jnp.float32), 'router_W': jax.random.normal(ks[1], (C, H, E), jnp.float32) * sd, 'router_b': jax.random.normal(ks[2], (C, E), jnp.float32) * sd, 'gate_bias': jax.random.normal(ks[3], (C, E), jnp.float32) * sd, 'exp_Wup': jax.random.normal(ks[4], (E, H, I), jnp.float32) * sd, 'exp_bup': jnp.zeros((E, I), jnp.float32), 'exp_Wg': jax.random.normal(ks[5], (E, I, I), jnp.float32) * sd, 'exp_bg': jnp.zeros((E, I), jnp.float32), 'exp_Wdown': jax.random.normal(ks[6], (E, I, H), jnp.float32) * sd, 'exp_bdown': jnp.zeros((E, H), jnp.float32), 'share_Wup': jax.random.normal(ks[7], (H, NS * I), jnp.float32) * sd, 'share_bup': jnp.zeros((NS * I,), jnp.float32), 'share_Wg': jax.random.normal(ks[8], (I, I), jnp.float32) * sd, 'share_bg': jnp.zeros((I,), jnp.float32), 'share_Wdown': jax.random.normal(ks[9], (I, H), jnp.float32) * sd, 'share_bdown': jnp.zeros((H,), jnp.float32), 'norm_w': jnp.ones((C, H), jnp.float32)}
        return inp
    _L1_ffn_in = _L1_ffn_setup()
    _d = {'L0_attn_x': _L0_attn_in['x'], 'L0_attn_rby': _L0_attn_in['rby'], 'L0_attn_Wq': _L0_attn_in['Wq'], 'L0_attn_bq': _L0_attn_in['bq'], 'L0_attn_Wk': _L0_attn_in['Wk'], 'L0_attn_bk': _L0_attn_in['bk'], 'L0_attn_Wv': _L0_attn_in['Wv'], 'L0_attn_bv': _L0_attn_in['bv'], 'L0_attn_Wo': _L0_attn_in['Wo'], 'L0_attn_bo': _L0_attn_in['bo'], 'L0_attn_ln_gamma': _L0_attn_in['ln_gamma'], 'L0_attn_ln_beta': _L0_attn_in['ln_beta'], 'L0_ffn_Wg': _L0_ffn_in['Wg'], 'L0_ffn_W1': _L0_ffn_in['W1'], 'L0_ffn_W2': _L0_ffn_in['W2'], 'L1_attn_qkv_w': _L1_attn_in['qkv_w'], 'L1_attn_qkv_b': _L1_attn_in['qkv_b'], 'L1_attn_proj_w': _L1_attn_in['proj_w'], 'L1_attn_proj_b': _L1_attn_in['proj_b'], 'L1_attn_projection_matrix': _L1_attn_in['projection_matrix'], 'L1_ffn_router_W': _L1_ffn_in['router_W'], 'L1_ffn_router_b': _L1_ffn_in['router_b'], 'L1_ffn_gate_bias': _L1_ffn_in['gate_bias'], 'L1_ffn_exp_Wup': _L1_ffn_in['exp_Wup'], 'L1_ffn_exp_bup': _L1_ffn_in['exp_bup'], 'L1_ffn_exp_Wg': _L1_ffn_in['exp_Wg'], 'L1_ffn_exp_bg': _L1_ffn_in['exp_bg'], 'L1_ffn_exp_Wdown': _L1_ffn_in['exp_Wdown'], 'L1_ffn_exp_bdown': _L1_ffn_in['exp_bdown'], 'L1_ffn_share_Wup': _L1_ffn_in['share_Wup'], 'L1_ffn_share_bup': _L1_ffn_in['share_bup'], 'L1_ffn_share_Wg': _L1_ffn_in['share_Wg'], 'L1_ffn_share_bg': _L1_ffn_in['share_bg'], 'L1_ffn_share_Wdown': _L1_ffn_in['share_Wdown'], 'L1_ffn_share_bdown': _L1_ffn_in['share_bdown'], 'L1_ffn_norm_w': _L1_ffn_in['norm_w']}
    _x0 = _d['L0_attn_x']
    _d['L0_attn_x'] = jax.random.normal(jax.random.fold_in(jax.random.key(seed), 1), (32, 256, 128), dtype=_x0.dtype)
    del _x0
    return _d

def reference(L0_attn_x, L0_attn_rby, L0_attn_Wq, L0_attn_bq, L0_attn_Wk, L0_attn_bk, L0_attn_Wv, L0_attn_bv, L0_attn_Wo, L0_attn_bo, L0_attn_ln_gamma, L0_attn_ln_beta, L0_ffn_Wg, L0_ffn_W1, L0_ffn_W2, L1_attn_qkv_w, L1_attn_qkv_b, L1_attn_proj_w, L1_attn_proj_b, L1_attn_projection_matrix, L1_ffn_router_W, L1_ffn_router_b, L1_ffn_gate_bias, L1_ffn_exp_Wup, L1_ffn_exp_bup, L1_ffn_exp_Wg, L1_ffn_exp_bg, L1_ffn_exp_Wdown, L1_ffn_exp_bdown, L1_ffn_share_Wup, L1_ffn_share_bup, L1_ffn_share_Wg, L1_ffn_share_bg, L1_ffn_share_Wdown, L1_ffn_share_bdown, L1_ffn_norm_w):

    def _L0_attn_ref(x, rby, Wq, bq, Wk, bk, Wv, bv, Wo, bo, ln_gamma, ln_beta):
        import jax, jax.numpy as jnp
        import numpy as np
        import math
        D_MODEL = 128
        N_HEADS = 16
        D_K = D_MODEL // N_HEADS
        BATCH = 4
        SEQ = 256
        TRAINING_PROGRESS = 0.25
        CONVERGENCE_PHASE = 0.5
        TENSION = abs(1.0 - 1.0)

        def _pos_encoding(seq_len, d, yellow):
            phase_mod = 0.1 * math.sin(2.0 * math.pi * TRAINING_PROGRESS)
            i_even = jnp.arange(0, d, 2, dtype=jnp.float32)
            denom = jnp.power(10000.0, 2.0 * i_even / d) * (1.0 + yellow * phase_mod)
            pos = jnp.arange(seq_len, dtype=jnp.float32)
            ang = pos[:, None] / denom[None, :]
            pe = jnp.zeros((seq_len, d), jnp.float32)
            pe = pe.at[:, 0::2].set(jnp.sin(ang))
            pe = pe.at[:, 1::2].set(jnp.cos(ang))
            return pe
        B, S, d = x.shape
        red, blue, yellow = (rby[0], rby[1], rby[2])
        x = x + _pos_encoding(S, d, yellow)[None, :, :]

        def proj(W, b):
            return (x @ W.T + b).reshape(B, S, N_HEADS, D_K).transpose(0, 2, 1, 3)
        Q, K, V = (proj(Wq, bq), proj(Wk, bk), proj(Wv, bv))
        scale = jnp.sqrt(D_K * (1.0 + TENSION * red))
        logits = jnp.einsum('bhqd,bhkd->bhqk', Q, K) / scale
        scale_matrix = 1.0 + red * 0.1 + blue * 0.05 + yellow * 0.15
        logits = logits * scale_matrix
        attn = jax.nn.softmax(logits, axis=-1)
        eps_adaptive = 0.1 * math.sin(2.0 * math.pi * CONVERGENCE_PHASE)
        out = jnp.einsum('bhqk,bhkd->bhqd', attn, V) * (1.0 + yellow * eps_adaptive)
        out = out.transpose(0, 2, 1, 3).reshape(B, S, d)
        out = out @ Wo.T + bo
        x = x + out
        mean = jnp.mean(x, axis=-1, keepdims=True)
        var = jnp.var(x, axis=-1, keepdims=True)
        eps_rby = 1e-05 * (1.0 + blue * 0.1)
        gamma_rby = ln_gamma * (1.0 + red * 0.1 + yellow * 0.05)
        normalized = (x - mean) / jnp.sqrt(var + eps_rby)
        return normalized * gamma_rby + ln_beta

    def _L0_ffn_ref(x, Wg, W1, W2):
        import jax, jax.numpy as jnp
        import numpy as np
        B, S, D = x.shape
        E = Wg.shape[1]
        T = B * S
        cap = max(1, T // E)
        xt = x.reshape(T, D)
        logits = xt @ Wg
        probs = jax.nn.softmax(logits, axis=-1)
        pT = probs.T
        _, top_idx = jax.lax.top_k(pT, cap)
        sel = jnp.zeros((E, T), dtype=bool).at[jnp.arange(E)[:, None], top_idx].set(True)
        masked = jnp.where(sel, pT, -jnp.inf)
        assigned = sel.any(axis=0)
        tok2exp = jnp.where(assigned, jnp.argmax(masked, axis=0), jnp.argmax(pT, axis=0))
        weights = jnp.take_along_axis(probs, tok2exp[:, None], axis=1)[:, 0]
        out = jnp.zeros_like(xt)
        for e in range(E):
            gate = jnp.where(tok2exp == e, weights, 0.0)
            h = jax.nn.gelu(xt @ W1[e], approximate=False) @ W2[e]
            out = out + gate[:, None] * h
        return out.reshape(B, S, D)

    def _L1_attn_ref(x, qkv_w, qkv_b, proj_w, proj_b, projection_matrix):
        import math
        import jax, jax.numpy as jnp
        import numpy as np
        B, N, D = (4, 512, 128)
        H, M = (16, 64)
        HD = D // H
        EPS = 1e-06

        def favor_features(data, proj):
            hd = data.shape[-1]
            m = proj.shape[0]
            dn = data / math.sqrt(hd)
            norm_sq = 0.5 * jnp.sum(dn * dn, axis=-1, keepdims=True)
            comb = jnp.einsum('bhnd,md->bhnm', dn, proj) - norm_sq
            comb = comb - jnp.max(comb, axis=-1, keepdims=True)
            return jnp.exp(comb) / math.sqrt(m) + EPS
        b, n, d = x.shape
        qkv = x @ qkv_w.T + qkv_b
        qkv = qkv.reshape(b, n, 3, H, HD)
        qkv = jnp.transpose(qkv, (2, 0, 3, 1, 4))
        q, k, v = (qkv[0], qkv[1], qkv[2])
        q_p = favor_features(q, projection_matrix)
        k_p = favor_features(k, projection_matrix)
        kv = jnp.einsum('bhnm,bhnv->bhmv', k_p, v)
        out = jnp.einsum('bhnm,bhmv->bhnv', q_p, kv)
        k_sum = jnp.sum(k_p, axis=2)
        normalizer = jnp.einsum('bhnm,bhm->bhn', q_p, k_sum)[..., None]
        out = out / (normalizer + EPS)
        out = jnp.transpose(out, (0, 2, 1, 3)).reshape(b, n, d)
        return out @ proj_w.T + proj_b

    def _L1_ffn_ref(x, router_W, router_b, gate_bias, exp_Wup, exp_bup, exp_Wg, exp_bg, exp_Wdown, exp_bdown, share_Wup, share_bup, share_Wg, share_bg, share_Wdown, share_bdown, norm_w):
        import jax, jax.numpy as jnp
        import numpy as np
        H, I, E, NS, C = (128, 128, 6, 2, 2)
        TOPK = 2
        TEMP = 1.0
        EPS = 1e-06
        B, S, Hd = x.shape
        xf = x.reshape(-1, Hd)
        for j in range(C):
            residual = xf
            gate = (xf @ router_W[j] + router_b[j]) / TEMP
            biased = gate + gate_bias[j]
            _, ids = jax.lax.top_k(biased, TOPK)
            sel = (ids[:, :, None] == jnp.arange(E)[None, None, :]).any(axis=1)
            weights = jax.nn.softmax(jnp.where(sel, gate, -jnp.inf), axis=-1)
            h = jnp.einsum('nh,ehi->eni', xf, exp_Wup) + exp_bup[:, None, :]
            h = jax.nn.silu(jnp.einsum('eni,eij->enj', h, exp_Wg) + exp_bg[:, None, :]) * h
            eo = jnp.einsum('eni,eih->enh', h, exp_Wdown) + exp_bdown[:, None, :]
            combined = jnp.einsum('ne,enh->nh', weights, eo)
            s = (xf @ share_Wup + share_bup).reshape(-1, NS, I)
            s = jax.nn.silu(s @ share_Wg + share_bg) * s
            share_out = (s @ share_Wdown + share_bdown).sum(axis=1)
            z = combined + share_out
            y = residual + z
            y = y * jax.lax.rsqrt(jnp.mean(y * y, axis=-1, keepdims=True) + EPS) * norm_w[j]
            xf = y
        return xf.reshape(B, S, Hd)
    x = L0_attn_x
    xn = _layernorm(x, axis=-1)
    x = x + _L0_attn_ref(xn, L0_attn_rby, L0_attn_Wq, L0_attn_bq, L0_attn_Wk, L0_attn_bk, L0_attn_Wv, L0_attn_bv, L0_attn_Wo, L0_attn_bo, L0_attn_ln_gamma, L0_attn_ln_beta) + _L0_ffn_ref(xn, L0_ffn_Wg, L0_ffn_W1, L0_ffn_W2)
    xn = _layernorm(x, axis=-1)
    x = x + _L1_attn_ref(xn, L1_attn_qkv_w, L1_attn_qkv_b, L1_attn_proj_w, L1_attn_proj_b, L1_attn_projection_matrix) + _L1_ffn_ref(xn, L1_ffn_router_W, L1_ffn_router_b, L1_ffn_gate_bias, L1_ffn_exp_Wup, L1_ffn_exp_bup, L1_ffn_exp_Wg, L1_ffn_exp_bg, L1_ffn_exp_Wdown, L1_ffn_exp_bdown, L1_ffn_share_Wup, L1_ffn_share_bup, L1_ffn_share_Wg, L1_ffn_share_bg, L1_ffn_share_Wdown, L1_ffn_share_bdown, L1_ffn_norm_w)
    return x

_drawn_inputs = setup_inputs


def setup_inputs(seed=0):
    import zlib

    import numpy as np

    out = dict(_drawn_inputs(seed))
    spreads = {'L0_attn_bq': (0.0, 0.8),
     'L0_attn_bk': (0.0, 2.0),
     'L0_attn_bv': (0.0, 0.725),
     'L0_attn_bo': (0.0, 0.1),
     'L0_attn_ln_gamma': (1.0, 0.2),
     'L0_attn_ln_beta': (0.0, 0.1),
     'L1_attn_qkv_b': (0.0, 0.1),
     'L1_attn_proj_b': (0.0, 0.1),
     'L1_ffn_exp_bup': (0.0, 0.8),
     'L1_ffn_exp_bg': (0.0, 0.8),
     'L1_ffn_exp_bdown': (0.0, 0.781),
     'L1_ffn_share_bup': (0.0, 0.8),
     'L1_ffn_share_bg': (0.0, 0.8),
     'L1_ffn_share_bdown': (0.0, 0.532),
     'L1_ffn_norm_w': (1.0, 0.2)}
    factors = {'L0_attn_Wq': 8.0,
     'L0_attn_Wk': 8.0,
     'L0_attn_Wv': 3.726,
     'L0_attn_Wo': 3.082,
     'L0_ffn_Wg': 8.0,
     'L0_ffn_W1': 8.0,
     'L0_ffn_W2': 8.0,
     'L1_attn_projection_matrix': 8.0,
     'L1_ffn_router_b': 7.54,
     'L1_ffn_gate_bias': 6.405,
     'L1_ffn_exp_Wup': 8.0,
     'L1_ffn_exp_Wg': 8.0,
     'L1_ffn_exp_Wdown': 8.0,
     'L1_ffn_share_Wup': 8.0,
     'L1_ffn_share_Wg': 8.0,
     'L1_ffn_share_Wdown': 8.0}
    for name, (base, spread) in spreads.items():
        noise = np.random.default_rng([zlib.crc32(name.encode()), seed]).standard_normal(out[name].shape)
        drawn = base * np.exp(spread * noise) if base else spread * noise
        out[name] = jnp.asarray(drawn.astype(out[name].dtype))
    for name, factor in factors.items():
        out[name] = (out[name] * factor).astype(out[name].dtype)
    return out
```

```python
import math
from contextlib import ExitStack

import concourse.bass as bass
from concourse import mybir

F32 = mybir.dt.float32
F32R = mybir.dt.float32r
I32 = mybir.dt.int32
ALU = mybir.AluOpType
ACT = mybir.ActivationFunctionType
AX = mybir.AxisListType

P = 128
SEQ = 256
BATCH = 32
TILES = BATCH * SEQ // P
GROUP = 4
CHUNK = 8
HEADS, HD = 16, 8
E0, F0 = 8, 256
CAP = BATCH * SEQ // E0
M = 64
E1, NS, CYCLES = 6, 2, 2
BASE = 32


FIELDS = [
    ("ident", 128), ("wg", 8),
    ("rev_expert", 8), ("bias_lo", 1), ("kv_mask", 256),
    ("qw", 128), ("kw", 128), ("proj", 1024), ("qkb", 4), ("vw", 128), ("vb", 128), ("pw", 128), ("pb", 128),
    ("router", 12), ("router_b", 12), ("gate_b", 12),
    ("up", 768), ("up_b", 6), ("gw", 768), ("gw_b", 6), ("down", 768), ("down_b", 128),
    ("s_up", 256), ("s_up_b", 2), ("s_gw", 128), ("s_gw_b", 1), ("s_down", 128), ("norm_w", 256),
]
FIRST = 128 + 8
FIELDS_0 = [
    ("same_expert", 128), ("before", 128), ("ones", 128), ("positions", 256),
    ("inv_base", 1), ("phase", 1), ("lo_q", 1), ("lo_k", 1), ("ones_k", 1),
    ("rby", 3), ("wq", 512), ("wk", 512), ("bq", 4), ("bk", 4), ("wv", 128), ("wo", 128),
    ("bv", 128), ("bo", 128), ("gamma", 128), ("beta", 128), ("w1", 2048), ("w2", 2048),
]


def columns(fields):
    at, found = 0, {}
    for name, width in fields:
        found[name] = (at, width)
        at += width
    return found, at


COLUMN, PACK = columns(FIELDS)
COLUMN_0, PACK_0 = columns(FIELDS_0)


class Core:
    pass


def field(core, name):
    if name in COLUMN:
        at, width = COLUMN[name]
        return core.pack[:, at:at + width]
    at, width = COLUMN_0[name]
    return core.pack_0[:, at:at + width]


class Chain:

    def __init__(self, eng, sem, base=0):
        self.eng, self.sem, self.base, self.n = eng, sem, base, 0

    def step(self, ins):
        self.n += 1
        return ins.then_inc(self.sem, 1)

    def link(self, ins):
        self.step(ins)
        self.eng.wait_ge(self.sem, self.base + self.n + BASE)


def based(nc, ctx, name):
    made = ctx.enter_context(nc.semaphore(name))
    nc.sync.sem_inc(made, BASE)
    return made


def carry_wait(core, eng):
    eng.sem_inc(core.passed, 1)


def product(pe, out, left, right, start=True, stop=True):
    (lh, ll), (rh, rl) = left, right
    pe.matmul(out, lh, rh, start=start, stop=False)
    pe.matmul(out, ll, rh, start=False, stop=False)
    return pe.matmul(out, lh, rl, start=False, stop=stop)


class Chunk:

    def __init__(self, half, par):
        self.n, self.half, self.par = 2 * half + par, half, par


def over_chunks(eng, first, body, last):
    halves = TILES // CHUNK // 2
    first(Chunk(0, 0))
    with eng.Fori(0, halves - 1) as i:
        body(Chunk(i, 0), Chunk(i, 1))
        body(Chunk(i, 1), Chunk(i + 1, 0))
    body(Chunk(halves - 1, 0), Chunk(halves - 1, 1))
    last(Chunk(halves - 1, 1))


def norm_block(nc, core, x_dram, pack_dram):
    with ExitStack() as ctx:
        sb = lambda name, shape, dt=F32: ctx.enter_context(nc.sbuf_tensor(name, shape, dt))
        sem = lambda name: based(nc, ctx, name)
        HALVES = CHUNK // GROUP
        xn = sb("n_xn", [P, 2, CHUNK, P])
        xnt = sb("n_xnt", [P, 2, HALVES, GROUP * P])
        stats = sb("n_stats", [P, 2, CHUNK, 6])
        mv = sb("n_mv", [P, 2, CHUNK, 2])
        ve = sb("n_ve", [P, CHUNK])
        rstd = sb("n_rstd", [P, 2, CHUNK])
        ps_t = [ctx.enter_context(nc.psum_tensor(f"n_ps_t{u}", [P, GROUP * P], F32)) for u in range(HALVES)]
        ps_l = [ctx.enter_context(nc.psum_tensor(f"n_ps_l{u}", [P, 512], F32)) for u in range(2)]
        w_first, w_in = sem("n_w_first"), sem("n_w_in")
        x_in = [sem("n_x_in_even"), sem("n_x_in_odd")]
        vec, half, pool_own = sem("n_vec"), sem("n_half"), sem("n_pool_own")
        mv_ready, rstd_ready, xn_ready, kept = sem("n_mv_ready"), sem("n_rstd_ready"), sem("n_xn_ready"), sem("n_kept")
        turned, xnt_ready, moved = sem("n_turned"), sem("n_xnt_ready"), sem("n_moved")
        logits_done, logits_kept = sem("n_logits_done"), sem("n_logits_kept")
        nc.all_engine_barrier()
        block = ctx.enter_context(nc.Block())
        ident = field(core, "ident")
        tiles_of = lambda c: bass.ds(c.n * CHUNK, CHUNK)

        @block.sync
        def _(sp):
            x_rows = x_dram.rearrange("(t p) d -> p t d", p=P)

            def load(c):
                sp.dma_start(core.x[:, tiles_of(c), :], x_rows[:, tiles_of(c), :]).then_inc(x_in[c.par], 16)

            sp.dma_start(core.pack[:, 0:FIRST], pack_dram[:, 0:FIRST]).then_inc(w_first, 16)
            load(Chunk(0, 0))
            load(Chunk(0, 1))
            with sp.Fori(0, TILES // CHUNK // 2 - 1) as i:
                for par in range(2):
                    sp.wait_ge(x_in[par], 16 * i + 16 + BASE)
                    carry_wait(core, sp)
                    load(Chunk(i + 1, par))
            sp.dma_start(core.pack_0[:, :], pack_dram[:, PACK:PACK + PACK_0]).then_inc(w_in, 16)
            sp.dma_start(core.pack[:, FIRST:PACK], pack_dram[:, FIRST:PACK]).then_inc(w_in, 16)
            sp.wait_ge(w_in, 32 + BASE)

        @block.gpsimd
        def _(pool):
            pool.memset(core.minus_half[:, :], -0.5).then_inc(half, 1)
            pool.wait_ge(half, 1 + BASE)

            def inverse_std(c):
                pool.wait_ge(mv_ready, CHUNK * c.n + CHUNK + BASE)
                pool.wait_ge(xn_ready, CHUNK * c.n - CHUNK + BASE)
                carry_wait(core, pool)
                pool.tensor_scalar(ve[:, :], mv[:, c.par, :, 1], 1e-5, None, ALU.add).then_inc(pool_own, 1)
                pool.wait_ge(pool_own, c.n + 1 + BASE)
                pool.tensor_tensor(rstd[:, c.par], ve[:, :], core.minus_half[:, 0:CHUNK], ALU.pow).then_inc(rstd_ready, 1)
                pool.wait_ge(rstd_ready, c.n + 1 + BASE)
                carry_wait(core, pool)
                pool.tensor_copy(core.mean[:, tiles_of(c)], mv[:, c.par, :, 0]).then_inc(kept, 1)
                pool.tensor_copy(core.rstd[:, tiles_of(c)], rstd[:, c.par]).then_inc(kept, 1)

            over_chunks(pool, inverse_std, lambda c, nxt: inverse_std(nxt), lambda c: None)

        @block.vector
        def _(dve):
            def moments(c):
                dve.wait_ge(x_in[c.par], 16 * c.half + 16 + BASE)
                for t in range(CHUNK):
                    dve.bn_stats(stats[:, c.par, t, :], core.x[:, c.n * CHUNK + t, :]).then_inc(vec, 1)
                dve.wait_ge(vec, CHUNK * c.n + CHUNK + BASE)
                dve.wait_ge(kept, 2 * c.n - 2 + BASE)
                carry_wait(core, dve)
                for t in range(CHUNK):
                    dve.bn_aggr(mv[:, c.par, t, :], stats[:, c.par, t, :]).then_inc(mv_ready, 1)

            def normalise(c):
                dve.wait_ge(rstd_ready, c.n + 1 + BASE)
                dve.wait_ge(turned, HALVES * c.n - HALVES + BASE)
                for t in range(CHUNK):
                    dve.tensor_scalar(xn[:, c.par, t, :], core.x[:, c.n * CHUNK + t, :], mv[:, c.par, t, 0:1],
                                      rstd[:, c.par, t:t + 1], ALU.subtract, ALU.mult).then_inc(xn_ready, 1)

            def body(c, nxt):
                moments(nxt)
                normalise(c)

            over_chunks(dve, moments, body, normalise)

        @block.scalar
        def _(act):
            def move(c):
                act.wait_ge(logits_done, c.n - 1 + BASE)
                for g in range(HALVES):
                    act.wait_ge(turned, HALVES * c.n + g + 1 + BASE)
                    act.activation(xnt[:, c.par, g], ps_t[g][:, :], ACT.Copy).then_inc(xnt_ready, 1)
                    act.activation(core.xnt[:, bass.ds((c.n * HALVES + g) * (GROUP * P), GROUP * P)], ps_t[g][:, :],
                                   ACT.Copy).then_inc(moved, 1)

            def keep(c):
                act.wait_ge(logits_done, c.n + 1 + BASE)
                act.activation(core.probs[:, tiles_of(c), :], ps_l[c.par][:, 0:CHUNK * E0].rearrange("p (t e) -> p t e", e=E0),
                               ACT.Copy).then_inc(logits_kept, 1)

            def body(c, nxt):
                move(nxt)
                keep(c)

            over_chunks(act, move, body, keep)

        @block.tensor
        def _(pe):
            pe.wait_ge(w_first, 16 + BASE)

            def turn(c):
                for g in range(HALVES):
                    pe.wait_ge(xn_ready, CHUNK * c.n + GROUP * (g + 1) + BASE)
                    pe.wait_ge(moved, HALVES * c.n - HALVES + g + 1 + BASE)
                    for t in range(GROUP):
                        last = pe.transpose(ps_t[g][:, t * P:(t + 1) * P], xn[:, c.par, GROUP * g + t, :], ident)
                    last.then_inc(turned, 1)

            def logits(c):
                pe.wait_ge(xnt_ready, HALVES * c.n + HALVES + BASE)
                pe.wait_ge(logits_kept, c.n - 1 + BASE)
                for t in range(CHUNK):
                    last = pe.matmul(ps_l[c.par][:, t * E0:(t + 1) * E0],
                                     xnt[:, c.par, t // GROUP, t % GROUP * P:(t % GROUP + 1) * P],
                                     field(core, "wg"), start=True, stop=True)
                last.then_inc(logits_done, 1)

            def body(c, nxt):
                turn(nxt)
                logits(c)

            over_chunks(pe, turn, body, logits)


def choice_block(nc, core):
    DIGITS = 3
    VALUE_BITS = 30
    with ExitStack() as ctx:
        sb = lambda name, shape, dt=F32: ctx.enter_context(nc.sbuf_tensor(name, shape, dt))
        sem = lambda name: based(nc, ctx, name)
        work = sb("c_work", [P, TILES, E0])
        row = sb("c_row", [P, TILES])
        row2 = sb("c_row2", [P, TILES])
        pt = sb("c_pt", [P, 512])
        junk = sb("c_junk", [P, DIGITS, 512])
        sel = sb("c_sel", [P, TILES, E0])
        tied = sb("c_tied", [P, TILES, E0])
        scan = sb("c_scan", [P, 2, TILES, E0])
        a = sb("c_a", [P, TILES, E0])
        count = sb("c_count", [P, DIGITS])
        bits_i = sb("c_bits_i", [P, DIGITS], I32)
        bit_f = sb("c_bit_f", [P, 1])
        cand_i = sb("c_cand_i", [P, DIGITS], I32)
        over_cap = sb("c_over_cap", [P, DIGITS])
        digit = sb("c_digit", [P, 1])
        hit_i = sb("c_hit_i", [P, 1], I32)
        best_i = sb("c_best_i", [P, 1], I32)
        left = sb("c_left", [P, 1])
        wide = sb("c_wide", [P, 2, P])
        limits = sb("c_limits", [P, 2, E0])
        ps = ctx.enter_context(nc.psum_tensor("c_ps", [P, 512], F32))
        ps_n = ctx.enter_context(nc.psum_tensor("c_ps_n", [P, 512], F32))
        vec, shifted, exped = sem("c_vec"), sem("c_shifted"), sem("c_exped")
        probs_ready, turned = sem("c_probs_ready"), sem("c_turned")
        counted, summed = sem("c_counted"), sem("c_summed")
        tied_ready, ranked = sem("c_tied_ready"), sem("c_ranked")
        counted1, summed1 = sem("c_counted1"), sem("c_summed1")
        chosen, back = sem("c_chosen"), sem("c_back")
        bits_own = sem("c_bits_own")
        nc.all_engine_barrier()
        block = ctx.enter_context(nc.Block())
        probs, ident = core.probs, field(core, "ident")
        flat = lambda t: t[:, :, :].rearrange("p t e -> p (t e)")
        over = lambda r: r[:, :].unsqueeze(2).broadcast_to([P, TILES, E0])
        STEPS = VALUE_BITS // 2

        @block.vector
        def _(dve):
            c = Chain(dve, vec)
            c.link(dve.tensor_reduce(row[:, :], probs[:, :, :], AX.X, ALU.max))
            dve.tensor_tensor(work[:, :, :], probs[:, :, :], over(row), ALU.subtract).then_inc(shifted, 1)
            dve.wait_ge(exped, 1 + BASE)
            c.link(dve.tensor_reduce(row[:, :], work[:, :, :], AX.X, ALU.add))
            c.link(dve.reciprocal(row2[:, :], row[:, :]))
            dve.tensor_tensor(probs[:, :, :], work[:, :, :], over(row2), ALU.mult).then_inc(probs_ready, 1)
            dve.wait_ge(turned, 1 + BASE)
            c.link(dve.tensor_copy(pt[:, :], ps[:, :]))
            c.step(dve.memset(best_i[:, :], 0))
            for m in range(DIGITS):
                c.step(dve.memset(bits_i[:, m:m + 1], (m + 1) << (VALUE_BITS - 2)))
            c.step(dve.memset(bit_f[:, :], float(1 << (VALUE_BITS - 2))))
            dve.wait_ge(vec, c.n + BASE)
            with dve.Fori(0, STEPS) as i:
                own = Chain(dve, bits_own, i * 6)
                own.link(dve.tensor_tensor(cand_i[:, :], best_i[:, :].broadcast_to([P, DIGITS]), bits_i[:, :],
                                           ALU.bitwise_or))
                for m in range(DIGITS):
                    dve.tensor_scalar(junk[:, m, :], pt[:, :], cand_i[:, m:m + 1].bitcast(F32), 0.0, ALU.is_ge, ALU.add,
                                      accum_out=count[:, m:m + 1]).then_inc(counted, 1)
                own.step(dve.tensor_scalar(bits_i[:, :], bits_i[:, :], 2, None, ALU.logical_shift_right))
                dve.wait_ge(summed, i + 1 + BASE)
                own.link(dve.tensor_scalar(over_cap[:, :], ps_n[:, 0:DIGITS], float(CAP), 0.0, ALU.is_ge, ALU.add,
                                           accum_out=digit[:, :]))
                own.link(dve.tensor_scalar(hit_i[:, :], digit[:, :], bit_f[:, 0:1], None, ALU.mult))
                own.step(dve.tensor_tensor(best_i[:, :], best_i[:, :], hit_i[:, :], ALU.bitwise_or))
                own.step(dve.tensor_scalar(bit_f[:, :], bit_f[:, :], 0.25, None, ALU.mult))
                dve.wait_ge(bits_own, i * 6 + 6 + BASE)
            dve.tensor_scalar(junk[:, 0, :], pt[:, :], best_i[:, :].bitcast(F32), 0.0, ALU.is_gt, ALU.add,
                              accum_out=count[:, 0:1]).then_inc(counted1, 1)
            c.link(dve.tensor_copy(wide[:, 0, :], best_i[:, :].bitcast(F32).broadcast_to([P, P])))
            dve.wait_ge(summed1, 1 + BASE)
            c.link(dve.tensor_scalar(left[:, :], ps_n[:, 0:1], -1.0, float(CAP), ALU.mult, ALU.add))
            dve.tensor_copy(wide[:, 1, :], left[:, :].broadcast_to([P, P])).then_inc(chosen, 1)
            dve.wait_ge(back, 1 + BASE)
            c.link(dve.tensor_copy(limits[:, :, :], ps[:, 0:2 * P].rearrange("p (a n) -> p a n", a=2)[:, :, 0:E0]))
            limit = lambda m: limits[:, m, :].unsqueeze(1).broadcast_to([P, TILES, E0])
            dve.tensor_tensor(tied[:, :, :], probs[:, :, :], limit(0), ALU.is_equal).then_inc(tied_ready, 1)
            c.link(dve.tensor_tensor(sel[:, :, :], probs[:, :, :], limit(0), ALU.is_gt))
            dve.wait_ge(ranked, 1 + BASE)
            c.link(dve.tensor_copy(flat(scan[:, 0]), ps_n[:, :]))
            for m in range(6):
                step, old, new = 1 << m, scan[:, m % 2], scan[:, (m + 1) % 2]
                c.step(dve.tensor_copy(new[:, 0:step, :], old[:, 0:step, :]))
                c.link(dve.tensor_tensor(new[:, step:TILES, :], old[:, step:TILES, :], old[:, 0:TILES - step, :], ALU.add))
            c.link(dve.tensor_tensor(flat(scan[:, 1]), flat(scan[:, 0]), ps_n[:, :], ALU.subtract))
            c.link(dve.tensor_tensor(flat(scan[:, 0]), flat(scan[:, 1]), ps[:, :], ALU.add))
            c.link(dve.tensor_tensor(a[:, :, :], scan[:, 0], limit(1), ALU.is_lt))
            c.link(dve.tensor_tensor(a[:, :, :], a[:, :, :], tied[:, :, :], ALU.mult))
            c.link(dve.tensor_tensor(sel[:, :, :], sel[:, :, :], a[:, :, :], ALU.add))
            c.link(dve.tensor_tensor(a[:, :, :], probs[:, :, :], sel[:, :, :], ALU.mult))
            c.link(dve.scalar_tensor_tensor(flat(a), flat(sel), -1.0, flat(a), ALU.add, ALU.add))
            c.link(dve.tensor_reduce(row[:, :], a[:, :, :], AX.X, ALU.max))
            c.link(dve.tensor_scalar(row[:, :], row[:, :], 0.0, -4.0, ALU.is_ge, ALU.mult))
            c.link(dve.tensor_tensor(work[:, :, :], probs[:, :, :], over(row), ALU.add))
            c.link(dve.tensor_tensor(a[:, :, :], a[:, :, :], work[:, :, :], ALU.max))
            c.link(dve.tensor_reduce(row[:, :], a[:, :, :], AX.X, ALU.max))
            c.link(dve.tensor_tensor(work[:, :, :], a[:, :, :], over(row), ALU.is_equal))
            c.link(dve.tensor_tensor(work[:, :, :], work[:, :, :],
                                     field(core, "rev_expert").unsqueeze(1).broadcast_to([P, TILES, E0]), ALU.mult))
            c.link(dve.tensor_reduce(row2[:, :], work[:, :, :], AX.X, ALU.max))
            c.link(dve.tensor_tensor(work[:, :, :], work[:, :, :], over(row2), ALU.is_equal))
            c.link(dve.tensor_tensor(core.gates[:, :, :], work[:, :, :], over(row), ALU.mult))

        @block.scalar
        def _(act):
            act.wait_ge(shifted, 1 + BASE)
            act.activation(work[:, :, :], work[:, :, :], ACT.Exp).then_inc(exped, 1)

        @block.tensor
        def _(pe):
            same = field(core, "same_expert")
            pe.wait_ge(probs_ready, 1 + BASE)
            for q in range(4):
                last = pe.transpose(ps[:, q * P:(q + 1) * P],
                                    probs[:, 16 * q:16 * q + 16, :].rearrange("p t e -> p (t e)"), ident)
            last.then_inc(turned, 1)
            with pe.Fori(0, STEPS) as i:
                pe.wait_ge(counted, DIGITS * i + DIGITS + BASE)
                pe.matmul(ps_n[:, 0:DIGITS], same, count[:, :], start=True, stop=True).then_inc(summed, 1)
            pe.wait_ge(counted1, 1 + BASE)
            pe.matmul(ps_n[:, 0:1], same, count[:, 0:1], start=True, stop=True).then_inc(summed1, 1)
            pe.wait_ge(chosen, 1 + BASE)
            for m in range(2):
                last = pe.transpose(ps[:, m * P:(m + 1) * P], wide[:, m, :], ident)
            last.then_inc(back, 1)
            pe.wait_ge(tied_ready, 1 + BASE)
            pe.matmul(ps[:, :], field(core, "before"), flat(tied), start=True, stop=True)
            pe.matmul(ps_n[:, :], field(core, "ones"), flat(tied), start=True, stop=True).then_inc(ranked, 1)


class Batch:

    def __init__(self, n, par):
        self.n, self.par = n, par


def over_periods(eng, slot):
    def period(b, at=lambda n: Batch(n, n % 2), steady=False):
        four = [at(b + d) if steady or 0 <= b + d < BATCH else None for d in (-1, 0, 1, 2)]
        for u in range(8):
            slot(u, *four)

    for b in (-2, -1, 0):
        period(b)
    with eng.Fori(0, (BATCH - 4) // 2) as i:
        for par in (1, 0):
            period(2 - par, lambda n: Batch(2 * i + n, n % 2), steady=True)
    for b in range(BATCH - 3, BATCH + 1):
        period(b)


USES = [["P0", "R4", "R5"], ["P1", "V0", "V1", "R6", "R7"], ["P2", "R8", "R9", "R10"], ["P3", "R11", "R12"],
        ["P4", "R13", "R14"], ["P5", "R15"], ["P6", "N0", "N1"], ["P7", "N2", "N3"]]


def uses(u, r, p):
    here = [[x for x in slot if (p if x[0] in "PN" else r)] for slot in USES]
    start = sum(len(slot) for slot in here[:u])
    return [(x[0], int(x[1:]), start + k) for k, x in enumerate(here[u])], [x for slot in here for x in slot]


def attention_block(nc, core):
    with ExitStack() as ctx:
        sb = lambda name, shape, dt=F32: ctx.enter_context(nc.sbuf_tensor(name, shape, dt))
        sem = lambda name: based(nc, ctx, name)
        pb = lambda name, cols: ctx.enter_context(nc.psum_tensor(name, [P, cols], F32))
        G = HEADS // 4
        pe_t = sb("a_pe_t", [P, SEQ])
        pe_bo = sb("a_pe_bo", [P, 2, P])
        ang = sb("a_ang", [P, SEQ])
        turns = sb("a_turns", [P, SEQ])
        small = sb("a_small", [P, 16])
        bq = sb("a_bq", [P, 4])
        bk = sb("a_bk", [P, 4])
        gamma = sb("a_gamma", [P, P])
        wo = sb("a_wo", [P, P])
        xpt = sb("a_xpt", [P, 2, SEQ])
        full = sb("a_full", [P, 2, SEQ])
        upper = sb("a_upper", [P, 2, SEQ], F32R)
        qs = sb("a_qs", [P, 2, G, SEQ], F32R)
        qm = sb("a_qm", [P, G, SEQ], F32R)
        ks = sb("a_ks", [P, G, SEQ], F32R)
        kz = sb("a_kz", [P, 2, G, 4, SEQ], F32R)
        vs = sb("a_vs", [P, 2, 2, HEADS, 32])
        mx = sb("a_mx", [P, 2, 2, HEADS])
        mx_hi = sb("a_mx_hi", [P, 2, HEADS], F32R)
        mrow = sb("a_mrow", [P, 2, HEADS, 32])
        ex = sb("a_ex", [P, 2, 4, SEQ])
        ot = sb("a_ot", [P, G, SEQ])
        rec = sb("a_rec", [P, 2, HEADS])
        at = sb("a_at", [P, 2, HEADS, HD])
        att = sb("a_att", [P, 2, P])
        xpb = sb("a_xpb", [P, 2, P])
        y = sb("a_y", [P, 2, P])
        st = sb("a_st", [P, 2, 6])
        mv = sb("a_mv", [P, 2, 2])
        ve = sb("a_ve", [P, 2])
        rstd = sb("a_rstd", [P, 2])
        z = sb("a_z", [P, 2, P])
        ps_a = [pb(f"a_ps_a{u}", 512) for u in range(2)]
        ps_s = [pb(f"a_ps_s{u}", 1024) for u in range(2)]
        ps_o = [pb(f"a_ps_o{u}", 512) for u in range(2)]
        setup, pe_ready, pe_turned = sem("a_setup"), sem("a_pe_ready"), sem("a_pe_turned")
        split, kz_in = sem("a_split"), [sem(f"a_kz_in{u}") for u in range(2)]
        kz_zero = sem("a_kz_zero")
        reduced, dve_set, zeroed = sem("a_reduced"), sem("a_dve_set"), sem("a_zeroed")
        xpt_ready, projected, full_ready = sem("a_xpt_ready"), sem("a_projected"), sem("a_full_ready")
        upper_ready = sem("a_upper_ready")
        v_made, v_ready = sem("a_v_made"), sem("a_v_ready")
        rows_made, max_done = sem("a_rows_made"), sem("a_max_done")
        mx_own, mrow_ready = sem("a_mx_own"), sem("a_mrow_ready")
        m_turned, qm_ready = sem("a_m_turned"), sem("a_qm_ready")
        scored, exped, av_done = sem("a_scored"), sem("a_exped"), sem("a_av_done")
        ot_ready = sem("a_ot_ready")
        o_turned, rec_ready, at_ready = sem("a_o_turned"), sem("a_rec_ready"), sem("a_at_ready")
        at_turned, att_ready, out_made = sem("a_at_turned"), sem("a_att_ready"), sem("a_out_made")
        xn_own, xpb_ready, y_ready = sem("a_xn_own"), sem("a_xpb_ready"), sem("a_y_ready")
        st_ready, mv_ready = sem("a_st_ready"), sem("a_mv_ready")
        ve_ready, rstd_ready, z_ready, z_own, stored = (sem("a_ve_ready"), sem("a_rstd_ready"), sem("a_z_ready"),
                                                        sem("a_z_own"), sem("a_stored"))
        nc.all_engine_barrier()
        block = ctx.enter_context(nc.Block())
        ident = field(core, "ident")
        rby = field(core, "rby")
        red, blue, yellow = rby[:, 0:1], rby[:, 1:2], rby[:, 2:3]
        factor, eps = small[:, 0:1], small[:, 1:2]
        TENSION = 0.0
        SIN_QUARTER = 0.1
        SIN_HALF = 0.1 * math.sin(2.0 * math.pi * 0.5)

        @block.gpsimd
        def _(pool):
            c = Chain(pool, setup)
            c.link(pool.memset(small[:, 8:9], -0.5))
            c.link(pool.tensor_scalar(small[:, 3:4], red, TENSION * HD, float(HD), ALU.mult, ALU.add))
            c.link(pool.tensor_tensor(small[:, 4:5], small[:, 3:4], small[:, 8:9], ALU.pow))
            c.link(pool.tensor_scalar(small[:, 5:6], red, 0.1, 1.0, ALU.mult, ALU.add))
            c.link(pool.tensor_scalar(small[:, 6:7], blue, 0.05, None, ALU.mult))
            c.link(pool.tensor_tensor(small[:, 5:6], small[:, 5:6], small[:, 6:7], ALU.add))
            c.link(pool.tensor_scalar(small[:, 6:7], yellow, 0.15, None, ALU.mult))
            c.link(pool.tensor_tensor(small[:, 5:6], small[:, 5:6], small[:, 6:7], ALU.add))
            c.link(pool.tensor_tensor(factor, small[:, 5:6], small[:, 4:5], ALU.mult))
            c.link(pool.tensor_scalar(bq[:, :], field(core, "bq"), factor, None, ALU.mult))
            c.link(pool.tensor_scalar(bk[:, :], field(core, "bk"), field(core, "ones_k"), None, ALU.add))
            c.link(pool.tensor_scalar(eps, blue, 1e-6, 1e-5, ALU.mult, ALU.add))
            c.link(pool.tensor_scalar(small[:, 5:6], red, 0.1, 1.0, ALU.mult, ALU.add))
            c.link(pool.tensor_scalar(small[:, 6:7], yellow, 0.05, None, ALU.mult))
            c.link(pool.tensor_tensor(small[:, 5:6], small[:, 5:6], small[:, 6:7], ALU.add))
            c.link(pool.tensor_scalar(gamma[:, :], field(core, "gamma"), small[:, 5:6], None, ALU.mult))
            c.link(pool.tensor_scalar(small[:, 6:7], yellow, SIN_HALF, 1.0, ALU.mult, ALU.add))
            c.link(pool.tensor_scalar(wo[:, :], field(core, "wo"), small[:, 6:7], None, ALU.mult))
            pool.wait_ge(pe_turned, 1 + BASE)

            def start(q):
                pool.wait_ge(projected, 8 * q.n - 8 + BASE)
                pool.wait_ge(v_made, 2 * q.n - 2 + BASE)
                carry_wait(core, pool)
                pool.tensor_tensor(xpt[:, q.par], core.xnt[:, bass.ds(q.n * SEQ, SEQ)], pe_t[:, :],
                                   ALU.add).then_inc(xpt_ready, 1)

            def upper_half(p, s):
                pool.wait_ge(full_ready, 8 * p.n + s + 1 + BASE)
                pool.wait_ge(split, 8 * p.n + s - 1 + BASE)
                carry_wait(core, pool)
                pool.tensor_copy(upper[:, s % 2], full[:, s % 2]).then_inc(upper_ready, 1)

            def residual(t):
                pool.wait_ge(dve_set, 1 + BASE)
                pool.wait_ge(y_ready, t.n + BASE)
                carry_wait(core, pool)
                own = Chain(pool, xn_own, 2 * t.n)
                two = bass.ds(2 * t.n, 2)
                own.link(pool.tensor_tensor(xpb[:, :, :], core.x[:, two, :],
                                            core.mean[:, two].unsqueeze(2).broadcast_to([P, 2, P]), ALU.subtract))
                own.link(pool.tensor_tensor(xpb[:, :, :], xpb[:, :, :],
                                            core.rstd[:, two].unsqueeze(2).broadcast_to([P, 2, P]), ALU.mult))
                pool.tensor_tensor(xpb[:, :, :], xpb[:, :, :], pe_bo[:, :, :], ALU.add).then_inc(xpb_ready, 1)

            def inverse_std(t):
                pool.wait_ge(mv_ready, 2 * t.n + 2 + BASE)
                carry_wait(core, pool)
                pool.tensor_scalar(ve[:, :], mv[:, :, 1], eps, None, ALU.add).then_inc(ve_ready, 1)
                pool.wait_ge(ve_ready, t.n + 1 + BASE)
                pool.tensor_tensor(rstd[:, :], ve[:, :], core.minus_half[:, 0:2], ALU.pow).then_inc(rstd_ready, 1)

            def finish(t):
                own = Chain(pool, z_own, 2 * t.n)
                pool.wait_ge(z_ready, 2 * t.n + 2 + BASE)
                own.link(pool.tensor_tensor(z[:, :, :], z[:, :, :], gamma[:, :].unsqueeze(1).broadcast_to([P, 2, P]), ALU.mult))
                own.link(pool.tensor_tensor(z[:, :, :], z[:, :, :],
                                            field(core, "beta").unsqueeze(1).broadcast_to([P, 2, P]), ALU.add))
                carry_wait(core, pool)
                pool.tensor_tensor(core.x[:, bass.ds(2 * t.n, 2), :], core.x[:, bass.ds(2 * t.n, 2), :], z[:, :, :],
                                   ALU.add).then_inc(stored, 1)

            def slot(u, t, b, r, p):
                if p:
                    upper_half(p, u)
                if t and u == 1:
                    residual(t)
                if t and u == 4:
                    inverse_std(t)
                if t and u == 5:
                    finish(t)
                if p and u == 6 and not (isinstance(p.n, int) and p.n == BATCH - 1):
                    start(Batch(p.n + 1, 1 - p.par))

            start(Batch(0, 0))
            pool.memset(mrow[:, :, :, :], 0.0).then_inc(zeroed, 1)
            pool.memset(vs[:, :, :, :, :], 0.0).then_inc(zeroed, 1)
            pool.wait_ge(zeroed, 2 + BASE)
            pool.memset(vs[:, :, :, :, HD:HD + 1], 1.0).then_inc(zeroed, 1)
            over_periods(pool, slot)

        @block.sync
        def _(sp):
            sp.wait_ge(kz_zero, 1 + G + BASE)
            with sp.Fori(0, BATCH // 2) as i:
                for par in range(2):
                    n = 2 * i + par
                    for pair in range(2):
                        two = slice(2 * pair, 2 * pair + 2)
                        sp.wait_ge(split, 8 * n + 2 * pair + 2 + BASE)
                        carry_wait(core, sp)
                        sp.wait_ge(scored, 8 * n - 12 + 4 * pair + BASE)
                        carry_wait(core, sp)
                        for j in range(4):
                            sp.dma_start(kz[32 * j:32 * j + 32, par, two, j, :].bitcast(F32),
                                         ks[32 * j:32 * j + 32, two, :].bitcast(F32)).then_inc(kz_in[pair], 16)
            for pair in range(2):
                sp.wait_ge(kz_in[pair], 64 * BATCH + BASE)

        @block.vector
        def _(dve):
            c = Chain(dve, reduced)
            c.link(dve.tensor_scalar(small[:, 9:10], yellow, SIN_QUARTER, 1.0, ALU.mult, ALU.add))
            c.link(dve.reciprocal(small[:, 10:11], small[:, 9:10]))
            c.link(dve.tensor_scalar(small[:, 11:12], field(core, "inv_base"), small[:, 10:11], None, ALU.mult))
            c.link(dve.tensor_scalar(ang[:, :], field(core, "positions"), small[:, 11:12], field(core, "phase"), ALU.mult, ALU.add))
            c.link(dve.tensor_scalar(turns[:, :], ang[:, :], 1.0 / (2.0 * math.pi), 12582912.0, ALU.mult, ALU.add))
            c.link(dve.tensor_scalar(turns[:, :], turns[:, :], -12582912.0, None, ALU.add))
            c.link(dve.scalar_tensor_tensor(ang[:, :], turns[:, :], -6.28125, ang[:, :], ALU.mult, ALU.add))
            c.link(dve.scalar_tensor_tensor(ang[:, :], turns[:, :], 6.28125 - 2.0 * math.pi, ang[:, :], ALU.mult, ALU.add))
            c.link(dve.tensor_scalar(ang[:, :], ang[:, :], 3.1415925, -3.1415925, ALU.min, ALU.max))
            dve.memset(kz[:, 0].bitcast(F32), 0.0).then_inc(kz_zero, 1)
            dve.wait_ge(pe_turned, 1 + BASE)
            dve.tensor_tensor(pe_bo[:, :, :], ps_a[0][:, 0:SEQ].rearrange("p (t d) -> p t d", t=2),
                              field(core, "bo").unsqueeze(1).broadcast_to([P, 2, P]), ALU.add).then_inc(dve_set, 1)

            def halve(p, s):
                g, isk = s % 4, s < 4
                dve.wait_ge(upper_ready, 8 * p.n + s + 1 + BASE)
                if s in (0, 2):
                    dve.wait_ge(kz_in[s // 2], 64 * p.n + BASE)
                out = ks[:, g] if isk else qs[:, p.par, g]
                dve.scalar_tensor_tensor(out, upper[:, s % 2].bitcast(F32), field(core, "lo_k" if isk else "lo_q"),
                                         full[:, s % 2], ALU.mult, ALU.add).then_inc(split, 1)

            def values(r, t, place):
                dve.wait_ge(zeroed, 3 + BASE)
                dve.wait_ge(v_made, 2 * r.n + t + 1 + BASE)
                dve.wait_ge(av_done, 8 * r.n - 8 + BASE)
                dve.tensor_tensor(vs[:, r.par, t, :, 0:HD], ps_a[place % 2][:, 0:P].rearrange("p (h d) -> p h d", d=HD),
                                  field(core, "bv").rearrange("p (h d) -> p h d", d=HD), ALU.add).then_inc(v_ready, 1)

            def maxima(r, s, place):
                g, t, jp = s // 4, s // 2 % 2, s % 2
                dve.wait_ge(rows_made, 16 * r.n + s + 1 + BASE)
                dve.tensor_reduce(mx[:, r.par, t, 4 * g + 2 * jp:4 * g + 2 * jp + 2],
                                  ps_a[place % 2][:, :].rearrange("p (h k) -> p h k", h=2), AX.X, ALU.max).then_inc(max_done, 1)

            def max_rows(r):
                dve.wait_ge(max_done, 16 * r.n + 16 + BASE)
                dve.tensor_scalar(mx_hi[:, :, :], mx[:, r.par], -1.0, None, ALU.mult).then_inc(mx_own, 1)
                dve.wait_ge(mx_own, r.n + 1 + BASE)
                dve.wait_ge(zeroed, 3 + BASE)
                dve.wait_ge(m_turned, 2 * r.n + BASE)
                dve.tensor_copy(mrow[:, :, :, 24], mx_hi[:, :, :].bitcast(F32)).then_inc(mrow_ready, 1)
                dve.scalar_tensor_tensor(mrow[:, :, :, 25], mx[:, r.par], -1.0, mx_hi[:, :, :].bitcast(F32),
                                         ALU.mult, ALU.subtract).then_inc(mrow_ready, 1)

            def fold(b, half):
                dve.wait_ge(m_turned, 2 * b.n + half + 1 + BASE)
                dve.wait_ge(scored, 8 * b.n - 4 + 4 * half + BASE)
                dve.tensor_tensor(qm[:, 2 * half:2 * half + 2, :], ps_o[0][:, :].rearrange("p (g q) -> p g q", g=2),
                                  qs[:, b.par, 2 * half:2 * half + 2, :].bitcast(F32), ALU.add).then_inc(qm_ready, 1)

            def norm(b, t):
                ps = ps_o[1][:, :].rearrange("p (h r) -> p h r", r=32)
                dve.wait_ge(o_turned, 2 * b.n + t + 1 + BASE)
                dve.reciprocal(rec[:, t, :], ps[:, :, HD]).then_inc(rec_ready, 1)
                dve.wait_ge(rec_ready, 2 * b.n + t + 1 + BASE)
                dve.wait_ge(at_turned, b.n + BASE)
                dve.tensor_tensor(at[:, t], ps[:, :, 0:HD], rec[:, t, :].unsqueeze(2).broadcast_to([P, HEADS, HD]),
                                  ALU.mult).then_inc(at_ready, 1)

            def sum_y(b):
                dve.wait_ge(xpb_ready, b.n + 1 + BASE)
                dve.wait_ge(out_made, b.n + 1 + BASE)
                dve.tensor_tensor(y[:, :, :], ps_o[1][:, 256:512].rearrange("p (t d) -> p t d", t=2), xpb[:, :, :],
                                  ALU.add).then_inc(y_ready, 1)
                dve.wait_ge(y_ready, b.n + 1 + BASE)
                for t in range(2):
                    dve.bn_stats(st[:, t, :], y[:, t]).then_inc(st_ready, 1)
                dve.wait_ge(st_ready, 2 * b.n + 2 + BASE)
                carry_wait(core, dve)
                for t in range(2):
                    dve.bn_aggr(mv[:, t, :], st[:, t, :]).then_inc(mv_ready, 1)

            def make_z(b):
                dve.wait_ge(rstd_ready, b.n + 1 + BASE)
                dve.wait_ge(stored, b.n + BASE)
                for t in range(2):
                    dve.tensor_scalar(z[:, t], y[:, t], mv[:, t, 0:1], rstd[:, t:t + 1],
                                      ALU.subtract, ALU.mult).then_inc(z_ready, 1)

            def slot(u, t, b, r, p):
                if not r and not t and u < G:
                    dve.memset(kz[:, 1, u].bitcast(F32), 0.0).then_inc(kz_zero, 1)
                if u == 0 and b:
                    fold(b, 1)
                if u == 0 and r:
                    halve(r, 7)
                for kind, s, place in uses(u, r, p)[0]:
                    if kind == "V":
                        values(r, s, place)
                    if kind in "RN":
                        maxima(r if kind == "R" else p, s, place)
                if u >= 1 and p:
                    halve(p, u - 1)
                if t and u < 2:
                    norm(t, u)
                if t and u == 3:
                    sum_y(t)
                if t and u == 5:
                    make_z(t)
                if r and u == 5:
                    max_rows(r)
                if r and u == 6:
                    fold(r, 0)

            over_periods(dve, slot)

        @block.scalar
        def _(act):
            act.wait_ge(reduced, 9 + BASE)
            act.activation(pe_t[:, :], ang[:, :], ACT.Sin).then_inc(pe_ready, 1)
            act.wait_ge(setup, 18 + BASE)

            def biased(p, s, place):
                g, isk = s % 4, s < 4
                act.wait_ge(projected, 8 * p.n + s + 1 + BASE)
                act.wait_ge(split, 8 * p.n + s - 1 + BASE)
                act.activation(full[:, s % 2], ps_a[place % 2][:, 0:SEQ], ACT.Identity,
                               bias=(bk if isk else bq)[:, g:g + 1], scale=1.0 if isk else factor).then_inc(full_ready, 1)

            def exp(b, u):
                act.wait_ge(scored, 8 * b.n + u + 1 + BASE)
                act.wait_ge(av_done, 8 * b.n + u - 1 + BASE)
                act.activation(ex[:, u % 2], ps_s[u % 2][:, :].rearrange("p (j q) -> p j q", j=4), ACT.Exp).then_inc(exped, 1)

            def move_o(b, half):
                act.wait_ge(av_done, 8 * b.n + 4 * half + 4 + BASE)
                act.wait_ge(o_turned, 2 * b.n + BASE)
                act.activation(ot[:, 2 * half:2 * half + 2], ps_o[half][:, :].rearrange("p (g q) -> p g q", g=2),
                               ACT.Copy).then_inc(ot_ready, 1)

            def move_at(t):
                act.wait_ge(at_turned, t.n + 1 + BASE)
                act.activation(att[:, :, :].rearrange("p t d -> p (t d)"), ps_o[1][:, 0:256], ACT.Copy).then_inc(att_ready, 1)

            def slot(u, t, b, r, p):
                if u == 0 and t:
                    move_o(t, 1)
                for kind, s, place in uses(u, r, p)[0]:
                    if kind == "P":
                        biased(p, s, place)
                if b:
                    exp(b, u)
                if u == 2 and t:
                    move_at(t)
                if u == 4 and b:
                    move_o(b, 0)

            over_periods(act, slot)

        @block.tensor
        def _(pe):
            pe.wait_ge(pe_ready, 1 + BASE)
            for t in range(2):
                last = pe.transpose(ps_a[0][:, t * P:(t + 1) * P], pe_t[:, t * P:(t + 1) * P], ident)
            last.then_inc(pe_turned, 1)
            pe.wait_ge(setup, 18 + BASE)
            pe.wait_ge(dve_set, 1 + BASE)

            def bank(r, p, place, order):
                if place >= 2:
                    kind, s = order[place - 2][0], int(order[place - 2][1:])
                    if kind == "P":
                        pe.wait_ge(full_ready, 8 * p.n + s + 1 + BASE)
                    if kind == "V":
                        pe.wait_ge(v_ready, 2 * r.n + s + 1 + BASE)
                    if kind in "RN":
                        pe.wait_ge(max_done, 16 * (r if kind == "R" else p).n + s + 1 + BASE)
                elif r:
                    pe.wait_ge(max_done, 16 * r.n + 3 + place + BASE)
                return ps_a[place % 2]

            def project(p, s, ps):
                g, w = s % 4, field(core, "wk" if s < 4 else "wq")
                pe.wait_ge(xpt_ready, p.n + 1 + BASE)
                pe.matmul(ps[:, 0:SEQ], w[:, g * P:(g + 1) * P], xpt[:, p.par], start=True, stop=True).then_inc(projected, 1)

            def values(r, t, ps):
                pe.matmul(ps[:, 0:P], xpt[:, r.par, t * P:(t + 1) * P], field(core, "wv"),
                          start=True, stop=True).then_inc(v_made, 1)

            def rows(r, s, ps):
                g, t, jp = s // 4, s // 2 % 2, s % 2
                if s % 4 == 0:
                    pe.wait_ge(split, 8 * r.n + 5 + g + BASE)
                    pe.wait_ge(kz_in[g // 2], 64 * r.n + 64 + BASE)
                pe.matmul(ps[:, :], qs[:, r.par, g, t * P:(t + 1) * P],
                          kz[:, r.par, g, 2 * jp:2 * jp + 2, :], start=True, stop=True).then_inc(rows_made, 1)

            def turn_max(r, half):
                pe.wait_ge(mrow_ready, 2 * r.n + 2 + BASE)
                if half == 0:
                    pe.wait_ge(ot_ready, 2 * r.n - 1 + BASE)
                else:
                    pe.wait_ge(qm_ready, 2 * r.n + 1 + BASE)
                for g in range(2):
                    for t in range(2):
                        h = 4 * (2 * half + g)
                        last = pe.transpose(ps_o[0][:, (2 * g + t) * P:(2 * g + t + 1) * P],
                                            mrow[:, t, h:h + 4, :].rearrange("p h r -> p (h r)"), ident)
                last.then_inc(m_turned, 1)

            def scores(b, u):
                g, kt = u // 2, u % 2
                pe.wait_ge(qm_ready, 2 * b.n + g // 2 + 1 + BASE)
                pe.wait_ge(exped, 8 * b.n + u - 1 + BASE)
                for j in range(4):
                    last = pe.matmul(ps_s[u % 2][:, j * SEQ:(j + 1) * SEQ], kz[:, b.par, g, j, kt * P:(kt + 1) * P],
                                     qm[:, g, :], start=True, stop=True)
                last.then_inc(scored, 1)

            def weighted(b, u):
                g, kt = u // 2, u % 2
                pe.wait_ge(exped, 8 * b.n + u + 1 + BASE)
                if u == 0:
                    pe.wait_ge(v_ready, 2 * b.n + 2 + BASE)
                    pe.wait_ge(qm_ready, 2 * b.n + 2 + BASE)
                if u == 4:
                    pe.wait_ge(y_ready, b.n + BASE)
                at_g = slice(SEQ * (g % 2), SEQ * (g % 2) + SEQ)
                for j in range(4):
                    last = pe.matmul(ps_o[g // 2][32 * j:32 * j + 32, at_g], vs[:, b.par, kt, 4 * g + j, :],
                                     ex[:, u % 2, j, :], start=kt == 0, stop=kt == 1)
                last.then_inc(av_done, 1)

            def turn_o(b, t):
                pe.wait_ge(ot_ready, 2 * b.n + 2 + BASE)
                if t == 1:
                    pe.wait_ge(at_ready, 2 * b.n + 1 + BASE)
                for g in range(G):
                    last = pe.transpose(ps_o[1][:, g * P:(g + 1) * P], ot[:, g, t * P:(t + 1) * P], ident)
                last.then_inc(o_turned, 1)

            def turn_at(b):
                pe.wait_ge(at_ready, 2 * b.n + 2 + BASE)
                for t in range(2):
                    last = pe.transpose(ps_o[1][:, t * P:(t + 1) * P], at[:, t].rearrange("p h d -> p (h d)"), ident)
                last.then_inc(at_turned, 1)

            def output(b):
                pe.wait_ge(att_ready, b.n + 1 + BASE)
                for t in range(2):
                    last = pe.matmul(ps_o[1][:, 256 + t * P:256 + (t + 1) * P], att[:, t], wo[:, :], start=True, stop=True)
                last.then_inc(out_made, 1)

            def slot(u, t, b, r, p):
                here, order = uses(u, r, p)
                if u == 0 and t:
                    weighted(t, 7)
                if u == 0 and b:
                    turn_max(b, 1)
                for kind, s, place in here:
                    if kind == "P":
                        project(p, s, bank(r, p, place, order))
                if b:
                    scores(b, u)
                for kind, s, place in here:
                    if kind == "V":
                        values(r, s, bank(r, p, place, order))
                    if kind in "RN":
                        rows(r if kind == "R" else p, s, bank(r, p, place, order))
                if u >= 1 and b:
                    weighted(b, u - 1)
                if t:
                    if u < 2:
                        turn_o(t, u)
                    if u == 2:
                        turn_at(t)
                    if u == 3:
                        output(t)
                if r and u == 6:
                    turn_max(r, 0)

            over_periods(pe, slot)


def expert_block(nc, core):
    with ExitStack() as ctx:
        sb = lambda name, shape, dt=F32: ctx.enter_context(nc.sbuf_tensor(name, shape, dt))
        sem = lambda name: based(nc, ctx, name)
        pb = lambda name, cols: ctx.enter_context(nc.psum_tensor(name, [P, cols], F32))
        N = GROUP * P
        hid = sb("e_hid", [P, 2, 2, N])
        w1_hi = sb("e_w1_hi", [P, E0, 2, P], F32R)
        w1_lo = sb("e_w1_lo", [P, E0, 2, P], F32R)
        x_hi = sb("e_x_hi", [P, 2, N], F32R)
        x_lo = sb("e_x_lo", [P, 2, N], F32R)
        acc = sb("e_acc", [P, 2, GROUP, P])
        gate = sb("e_gate", [P, 2, GROUP, E0])
        ps_h = [pb(f"e_ps_h{u}", 512) for u in range(4)]
        ps_y = [pb(f"e_ps_y{u}", 512) for u in range(2)]
        gate_ready, h_made, h_ready, y_made = sem("e_gate_ready"), sem("e_h_made"), sem("e_h_ready"), sem("e_y_made")
        acc_step, stored = sem("e_acc_step"), sem("e_stored")
        w_hi_ready, w_lo_ready, x_hi_ready, x_lo_ready = (sem("e_w_hi_ready"), sem("e_w_lo_ready"), sem("e_x_hi_ready"),
                                                          sem("e_x_lo_ready"))
        nc.all_engine_barrier()
        block = ctx.enter_context(nc.Block())
        ROUNDS = TILES // GROUP // 2
        w1 = field(core, "w1").rearrange("p (e f n) -> p e f n", e=E0, f=2)
        w2 = field(core, "w2").rearrange("p (e f n) -> p e f n", e=E0, f=2)

        @block.gpsimd
        def _(pool):
            with pool.Fori(0, ROUNDS) as i:
                for u in range(2):
                    n = 2 * i + u
                    group = core.xnt[:, bass.ds(n * N, N)]
                    pool.wait_ge(h_made, 16 * n - 16 + BASE)
                    carry_wait(core, pool)
                    pool.tensor_copy(x_hi[:, u], group).then_inc(x_hi_ready, 1)
                    pool.wait_ge(x_hi_ready, n + 1 + BASE)
                    carry_wait(core, pool)
                    pool.tensor_tensor(x_lo[:, u], group, x_hi[:, u].bitcast(F32), ALU.subtract).then_inc(x_lo_ready, 1)

        @block.tensor
        def _(pe):
            def hidden(n, n_side, e):
                pe.wait_ge(x_lo_ready, n + 1 + BASE)
                for f in range(2):
                    pe.wait_ge(h_ready, (16 * n + 2 * e + f - 3 if e >= 2 else 16 * n) + BASE)
                    product(pe, ps_h[2 * (e % 2) + f][:, :], (w1_hi[:, e, f, :], w1_lo[:, e, f, :]),
                            (x_hi[:, n_side], x_lo[:, n_side])).then_inc(h_made, 1)

            def output(n, e):
                pe.wait_ge(h_ready, 16 * n + 2 * e + 2 + BASE)
                pe.wait_ge(acc_step, (32 * n + 4 * e - 4 if e >= 1 else 32 * n) + BASE)
                for t in range(GROUP):
                    for f in range(2):
                        last = pe.matmul(ps_y[e % 2][:, t * P:(t + 1) * P], hid[:, e % 2, f, t * P:(t + 1) * P],
                                         w2[:, e, f, :], start=f == 0, stop=f == 1)
                last.then_inc(y_made, 1)

            pe.wait_ge(w_lo_ready, E0 + BASE)
            with pe.Fori(0, ROUNDS) as i:
                for u in range(2):
                    n = 2 * i + u
                    for e in range(E0 + 1):
                        if e < E0:
                            hidden(n, u, e)
                        if e >= 1:
                            output(n, e - 1)

        @block.scalar
        def _(act):
            with act.Fori(0, ROUNDS) as i:
                for u in range(2):
                    n = 2 * i + u
                    for e in range(E0):
                        for f in range(2):
                            act.wait_ge(h_made, 16 * n + 2 * e + f + 1 + BASE)
                            act.wait_ge(y_made, (8 * n + e - 1 if e >= 2 else 8 * n) + BASE)
                            act.activation(hid[:, e % 2, f, :], ps_h[2 * (e % 2) + f][:, :], ACT.Gelu).then_inc(h_ready, 1)

        @block.vector
        def _(dve):
            for e in range(E0):
                dve.tensor_copy(w1_hi[:, e], w1[:, e]).then_inc(w_hi_ready, 1)
            for e in range(E0):
                dve.wait_ge(w_hi_ready, e + 1 + BASE)
                dve.tensor_tensor(w1_lo[:, e], w1[:, e], w1_hi[:, e].bitcast(F32), ALU.subtract).then_inc(w_lo_ready, 1)
            with dve.Fori(0, ROUNDS) as i:
                for u in range(2):
                    n = 2 * i + u
                    dve.tensor_copy(gate[:, u], core.gates[:, bass.ds(n * GROUP, GROUP), :]).then_inc(gate_ready, 1)
                    dve.wait_ge(gate_ready, n + 1 + BASE)
                    for e in range(E0):
                        dve.wait_ge(y_made, 8 * n + e + 1 + BASE)
                        for t in range(GROUP):
                            ps, out, g = ps_y[e % 2][:, t * P:(t + 1) * P], acc[:, u, t, :], gate[:, u, t, e:e + 1]
                            if e == 0:
                                ins = dve.tensor_scalar(out, ps, g, None, ALU.mult)
                            else:
                                dve.wait_ge(acc_step, 32 * n + 4 * e - 3 + t + BASE)
                                ins = dve.scalar_tensor_tensor(out, ps, g, out, ALU.mult, ALU.add)
                            ins.then_inc(acc_step, 1)
                    dve.wait_ge(acc_step, 32 * n + 32 + BASE)
                    x = core.x[:, bass.ds(n * GROUP, GROUP), :]
                    dve.tensor_tensor(x, x, acc[:, u], ALU.add).then_inc(stored, 1)


def second_block(nc, core, out_dram):
    with ExitStack() as ctx:
        sb = lambda name, shape, dt=F32: ctx.enter_context(nc.sbuf_tensor(name, shape, dt))
        sem = lambda name: based(nc, ctx, name)
        pb = lambda name, cols: ctx.enter_context(nc.psum_tensor(name, [P, cols], F32))
        N = GROUP * P
        C = HEADS // 2
        STEPS = NS + E1
        SUMS = GROUP * (E1 + 1)
        EPS = 1e-6
        SCALE = 1.0 / math.sqrt(HD)
        SET_DVE, SET_POOL = 13, 13
        stats = sb("s_stats", [P, GROUP, 6])
        mv = sb("s_mv", [P, GROUP, 2])
        ve = sb("s_ve", [P, GROUP])
        rstd = sb("s_rstd", [P, GROUP])
        cur = sb("s_cur", [P, 2, CYCLES + 1, GROUP, P])
        curt = sb("s_curt", [P, 2, CYCLES, N])
        x_hi = sb("s_x_hi", [P, 2, CYCLES, N], F32R)
        x_lo = sb("s_x_lo", [P, 2, CYCLES, N], F32R)
        up_hi = sb("s_up_hi", [P, STEPS, P], F32R)
        up_lo = sb("s_up_lo", [P, STEPS, P], F32R)
        gate_hi = sb("s_gate_hi", [P, STEPS, P], F32R)
        gate_lo = sb("s_gate_lo", [P, STEPS, P], F32R)
        gate_b = sb("s_gate_b", [P, STEPS])
        half_b = sb("s_half_b", [P, STEPS])
        h = sb("s_h", [P, 4, N])
        th = sb("s_th", [P, 2, N])
        h2 = sb("s_h2", [P, 2, N])
        acc = sb("s_acc", [P, 2, GROUP, P])
        down = sb("s_down", [P, STEPS - 1, P])
        msq = sb("s_msq", [P, GROUP])
        rms = sb("s_rms", [P, GROUP])
        sq = sb("s_sq", [P, P])
        g = sb("s_g", [P, GROUP, E1])
        gb = sb("s_gb", [P, GROUP, E1])
        eq = sb("s_eq", [P, GROUP, E1])
        first = sb("s_first", [P, GROUP, E1])
        second = sb("s_second", [P, GROUP, E1])
        top = sb("s_top", [P, GROUP])
        w = sb("s_w", [P, 2, GROUP, 8])
        wt = sb("s_wt", [8, N])
        wp_hi = sb("s_wp_hi", [P, 2, HEADS * M], F32R)
        wp_lo = sb("s_wp_lo", [P, 2, HEADS * M], F32R)
        bp = sb("s_bp", [2, 2, HEADS * M], F32R)
        bp_hi = sb("s_bp_hi", [2, 2, HEADS * M], F32R)
        one_f = sb("s_one_f", [2, P])
        ones = sb("s_ones", [2, P], F32R)
        v = sb("s_v", [P, 2, 2, C, 32])
        fmax = sb("s_fmax", [P, 2, HEADS])
        feat = sb("s_feat", [P, 4, HEADS * M])
        qpt = sb("s_qpt", [P, C, 2, P])
        kvt = sb("s_kvt", [P, 2, P])
        kv = sb("s_kv", [P, C, 32])
        ot = sb("s_ot", [P, 2, 2, P])
        den = sb("s_den", [P, 2, HEADS])
        rec = sb("s_rec", [P, 2, HEADS])
        at = sb("s_at", [P, 2, P])
        att = sb("s_att", [P, 2, P])
        res = sb("s_res", [P, 2, GROUP, P])
        ps_c = pb("s_ps_c", 1024)
        ps_m = pb("s_ps_m", 512)
        ps_u = pb("s_ps_u", 512)
        ps_g = [pb(f"s_ps_g{u}", 512) for u in range(2)]
        ps_d = pb("s_ps_d", 512)
        ps_n = pb("s_ps_n", 512)
        set_pool, set_pe, set_dve, set_act = sem("s_set_pool"), sem("s_set_pe"), sem("s_set_dve"), sem("s_set_act")
        st_ready, mv_ready, ve_ready, rstd_ready = sem("s_st_ready"), sem("s_mv_ready"), sem("s_ve_ready"), sem("s_rstd_ready")
        xn_ready, cur_ready = sem("s_xn_ready"), sem("s_cur_ready")
        c_made, c_read = sem("s_c_made"), sem("s_c_read")
        up_made, h_ready, gate_made, th_ready = sem("s_up_made"), sem("s_h_ready"), sem("s_gate_made"), sem("s_th_ready")
        th_own, h2_ready, down_made, acc_step = sem("s_th_own"), sem("s_h2_ready"), sem("s_down_made"), sem("s_acc_step")
        p_ready = sem("s_p_ready")
        route, tanh_in, tanh_out, w_ready = sem("s_route"), sem("s_tanh_in"), sem("s_tanh_out"), sem("s_w_ready")
        z_made, msq_ready, rms_own, rms_ready = sem("s_z_made"), sem("s_msq_ready"), sem("s_rms_own"), sem("s_rms_ready")
        v_ready, f_own, exped, k_ready = sem("s_v_ready"), sem("s_f_own"), sem("s_exped"), sem("s_k_ready")
        o_own = sem("s_o_own")
        hi_ready, lo_ready = sem("s_hi_ready"), sem("s_lo_ready")
        res_ready, fin_done, written = sem("s_res_ready"), sem("s_fin_done"), sem("s_written")
        JOBS = ("TURN", "GATE", "V", "WT", "KVT", "KV", "OT", "O", "AT", "OUT")
        TURN, GATE, V, WT, KVT, KV, OT, O, AT, OUT = range(len(JOBS))
        made = [sem(f"s_made_{name}") for name in JOBS]
        read = [sem(f"s_read_{name}") for name in JOBS]
        nc.all_engine_barrier()
        block = ctx.enter_context(nc.Block())
        ident = field(core, "ident")
        GROUPS = TILES // GROUP
        TAIL = 5
        CJ = 6
        K0, Q0, K1, TQ0, Q1, TQ1 = range(CJ)
        FEATURES = [(K0, 0, 0), (Q0, 1, 0), (K1, 0, 1), (Q1, 1, 1)]
        tiles = lambda t: slice(t * P, (t + 1) * P)
        weights = lambda name: field(core, name).rearrange("p (e n) -> p e n", n=P)
        up_w, gw_w = weights("up"), weights("gw")
        def step(x):
            if x < NS:
                return (weights("s_up")[:, x, :], field(core, "s_up_b")[:, x:x + 1], field(core, "s_gw"),
                        field(core, "s_gw_b"), E1)
            e = x - NS
            return up_w[:, e, :], field(core, "up_b")[:, e:e + 1], gw_w[:, e, :], field(core, "gw_b")[:, e:e + 1], e

        class Run:

            def __init__(self, i, j):
                self.b, self.j = 4 * i + j, j
                self.side, self.cyc = j % 2, j // 2
                self.group = 2 * i + self.side

        def over_runs(eng, head, slot):
            def window(run, nxt, then):
                for k in range(TAIL, STEPS):
                    slot(k, None, run, nxt)
                for k in range(TAIL):
                    slot(k, run, nxt, then)

            start = Run(0, 0)
            head(start)
            for k in range(TAIL):
                slot(k, None, start, Run(0, 1))
            with eng.Fori(0, GROUPS // 2 - 1) as i:
                for j in range(4):
                    window(Run(i, j), *[Run(i, m) if m < 4 else Run(i + 1, m - 4) for m in (j + 1, j + 2)])
            end = GROUPS // 2 - 1
            for j in range(4):
                window(Run(end, j), *[Run(end, m) if m < 4 else None for m in (j + 1, j + 2)])

        def behind(k, lag, prev, run):
            return (run, k - lag) if k >= lag else (prev, k - lag + STEPS)

        @block.gpsimd
        def _(pool):
            c = Chain(pool, set_pool)
            c.step(pool.tensor_scalar(down[:, 0:E1, :], weights("down"), 0.5, None, ALU.mult))
            c.step(pool.tensor_scalar(down[:, E1, :], field(core, "s_down"), 0.5, None, ALU.mult))
            c.link(pool.memset(v[:, :, :, :, :], 0.0))
            c.step(pool.memset(v[:, :, :, :, HD:HD + 1], 1.0))
            c.step(pool.memset(v[:, :, :, :, 2 * HD + 1:2 * HD + 2], 1.0))
            c.link(pool.memset(w[:, :, :, :], 0.0))
            c.step(pool.memset(w[:, :, :, E1:E1 + 1], float(NS)))
            c.link(pool.memset(one_f[:, :], 1.0))
            c.link(pool.tensor_copy(ones[:, :], one_f[:, :]))
            for to, x in ((slice(0, NS), weights("s_up")), (slice(NS, STEPS), up_w)):
                c.link(pool.tensor_copy(up_hi[:, to, :], x))
                c.link(pool.tensor_tensor(up_lo[:, to, :], x, up_hi[:, to, :].bitcast(F32), ALU.subtract))

            def silu(r, x):
                pool.wait_ge(h_ready, 8 * r.b + x + 1 + BASE)
                pool.wait_ge(th_ready, 8 * r.b + x + 1 + BASE)
                pool.tensor_tensor(th[:, x % 2], th[:, x % 2], h[:, x % 4], ALU.mult).then_inc(p_ready, 1)

            def inverse_std(r):
                pool.wait_ge(mv_ready, 4 * r.group + 4 + BASE)
                carry_wait(core, pool)
                pool.tensor_scalar(ve[:, :], mv[:, :, 1], 1e-5, None, ALU.add).then_inc(ve_ready, 1)
                pool.wait_ge(ve_ready, r.group + 1 + BASE)
                pool.tensor_tensor(rstd[:, :], ve[:, :], core.minus_half[:, 0:GROUP], ALU.pow).then_inc(rstd_ready, 1)

            def halve(r):
                pool.wait_ge(read[TURN], r.b + 1 + BASE)
                carry_wait(core, pool)
                pool.tensor_copy(x_hi[:, r.side, r.cyc], curt[:, r.side, r.cyc]).then_inc(hi_ready, 1)
                pool.wait_ge(hi_ready, r.b + 1 + BASE)
                pool.tensor_tensor(x_lo[:, r.side, r.cyc], curt[:, r.side, r.cyc], x_hi[:, r.side, r.cyc].bitcast(F32),
                                   ALU.subtract).then_inc(lo_ready, 1)

            def head(r):
                inverse_std(r)
                halve(r)

            def slot(k, prev, run, nxt):
                r, x = behind(k, 1, prev, run)
                if r:
                    silu(r, x)
                if k == 5 and nxt:
                    halve(nxt)
                if k == 2 and nxt and nxt.cyc == 0:
                    inverse_std(nxt)
                if k == 2 and prev:
                    pool.wait_ge(msq_ready, 4 * prev.b + 4 + BASE)
                    carry_wait(core, pool)
                    pool.tensor_scalar(msq[:, :], msq[:, :], 1.0 / P, EPS, ALU.mult, ALU.add).then_inc(rms_own, 1)
                    pool.wait_ge(rms_own, prev.b + 1 + BASE)
                    pool.tensor_tensor(rms[:, :], msq[:, :], core.minus_half[:, 0:GROUP], ALU.pow).then_inc(rms_ready, 1)
                if k == 4 and prev and prev.cyc == 1:
                    pool.wait_ge(cur_ready, 4 * prev.b + 4 + BASE)
                    pool.wait_ge(read[OUT], prev.b + 1 + BASE)
                    pool.tensor_tensor(res[:, prev.side], res[:, prev.side], cur[:, prev.side, CYCLES],
                                       ALU.add).then_inc(fin_done, 1)
                if k == 7 and run.cyc == 0:
                    pool.wait_ge(written, 16 * run.group - 16 + BASE)
                    carry_wait(core, pool)
                    pool.tensor_tensor(res[:, run.side], core.x[:, bass.ds(run.group * GROUP, GROUP), :],
                                       field(core, "pb").unsqueeze(1).broadcast_to([P, GROUP, P]),
                                       ALU.add).then_inc(res_ready, 1)

            over_runs(pool, head, slot)

        @block.sync
        def _(sp):
            out = out_dram.rearrange("(t p) d -> p t d", p=P)
            with sp.Fori(0, GROUPS // 2) as i:
                for side in range(2):
                    sp.wait_ge(fin_done, 2 * i + side + 1 + BASE)
                    carry_wait(core, sp)
                    sp.dma_start(out[:, bass.ds((2 * i + side) * GROUP, GROUP), :], res[:, side]).then_inc(written, 16)
                    sp.wait_ge(written, 16 * (2 * i + side) + 16 + BASE)
                    carry_wait(core, sp)
            sp.wait_ge(written, 16 * GROUPS + BASE)

        @block.vector
        def _(dve):
            c = Chain(dve, set_dve)
            dve.wait_ge(set_pe, 1 + BASE)
            c.step(dve.tensor_scalar(wp_hi[:, 0, :], ps_c[:, :], SCALE, None, ALU.mult))
            dve.wait_ge(set_dve, 1 + BASE)
            c.step(dve.scalar_tensor_tensor(wp_lo[:, 0, :], ps_c[:, :], SCALE, wp_hi[:, 0, :].bitcast(F32),
                                            ALU.mult, ALU.subtract))
            dve.wait_ge(set_act, 2 + 8 + BASE)
            for i in range(2):
                c.step(dve.scalar_tensor_tensor(bp[:, i, :], bp_hi[:, i, :].bitcast(F32), field(core, "bias_lo")[0:2, :],
                                                feat[0:2, 2 + i, :], ALU.mult, ALU.add))
            dve.wait_ge(set_pe, 5 + BASE)
            c.link(dve.tensor_scalar(wp_hi[:, 1, :], ps_c[:, :], SCALE, None, ALU.mult))
            c.step(dve.scalar_tensor_tensor(wp_lo[:, 1, :], ps_c[:, :], SCALE, wp_hi[:, 1, :].bitcast(F32),
                                            ALU.mult, ALU.subtract))
            dve.wait_ge(set_pe, 6 + BASE)
            for half, ps in enumerate((ps_m, ps_n)):
                to, gates = slice(4 * half, 4 * half + 4), ps[:, :].rearrange("p (x n) -> p x n", n=P)
                c.link(dve.tensor_copy(gate_hi[:, to, :], gates))
                c.step(dve.tensor_tensor(gate_lo[:, to, :], gates, gate_hi[:, to, :].bitcast(F32), ALU.subtract))
            c.step(dve.tensor_tensor(gate_b[:, NS:STEPS], ps_u[:, NS:STEPS], field(core, "gw_b"), ALU.add))
            c.link(dve.tensor_scalar(gate_b[:, 0:NS], ps_u[:, 0:NS], field(core, "s_gw_b"), None, ALU.add))
            c.link(dve.tensor_scalar(half_b[:, :], gate_b[:, :], 0.5, None, ALU.mult))
            assert c.n == SET_DVE, c.n
            dve.wait_ge(set_pool, SET_POOL + BASE)

            def best(own, out):
                rev = field(core, "rev_expert")[:, 0:E1].unsqueeze(1).broadcast_to([P, GROUP, E1])
                over_top = top[:, :].unsqueeze(2).broadcast_to([P, GROUP, E1])
                own.link(dve.tensor_reduce(top[:, :], gb[:, :, :], AX.X, ALU.max))
                own.link(dve.tensor_tensor(eq[:, :, :], gb[:, :, :], over_top, ALU.is_equal))
                own.link(dve.tensor_tensor(eq[:, :, :], eq[:, :, :], rev, ALU.mult))
                own.link(dve.tensor_reduce(top[:, :], eq[:, :, :], AX.X, ALU.max))
                own.link(dve.tensor_tensor(out, eq[:, :, :], over_top, ALU.is_equal))

            def logits(r):
                wide = field(core, "router_b")[:, r.cyc * E1:(r.cyc + 1) * E1].unsqueeze(1).broadcast_to([P, GROUP, E1])
                dve.wait_ge(made[GATE], r.b + 1 + BASE)
                dve.tensor_tensor(g[:, :, :], ps_m[:, 0:GROUP * E1].rearrange("p (t e) -> p t e", e=E1), wide,
                                  ALU.add).then_inc(read[GATE], 1)

            def router(r):
                own = Chain(dve, route, 15 * r.b)
                wide = field(core, "gate_b")[:, r.cyc * E1:(r.cyc + 1) * E1].unsqueeze(1).broadcast_to([P, GROUP, E1])
                dve.wait_ge(read[GATE], r.b + 1 + BASE)
                own.link(dve.tensor_tensor(gb[:, :, :], g[:, :, :], wide, ALU.add))
                best(own, first[:, :, :])
                own.link(dve.scalar_tensor_tensor(gb[:, :, :], first[:, :, :], -3e38, gb[:, :, :], ALU.mult, ALU.add))
                best(own, second[:, :, :])
                own.link(dve.tensor_tensor(eq[:, :, :], first[:, :, :], second[:, :, :], ALU.subtract))
                own.link(dve.tensor_tensor(gb[:, :, :], g[:, :, :], eq[:, :, :], ALU.mult))
                dve.tensor_reduce(top[:, :], gb[:, :, :], AX.X, ALU.add).then_inc(tanh_in, 1)

            def routed(r):
                own = Chain(dve, route, 15 * r.b + 14)
                dve.wait_ge(tanh_out, r.b + 1 + BASE)
                own.link(dve.tensor_tensor(eq[:, :, :], eq[:, :, :], top[:, :].unsqueeze(2).broadcast_to([P, GROUP, E1]), ALU.mult))
                dve.tensor_tensor(gb[:, :, :], first[:, :, :], second[:, :, :], ALU.add).then_inc(w_ready, 1)
                dve.wait_ge(w_ready, 3 * r.b + 1 + BASE)
                dve.tensor_tensor(gb[:, :, :], gb[:, :, :], eq[:, :, :], ALU.add).then_inc(w_ready, 1)
                dve.wait_ge(w_ready, 3 * r.b + 2 + BASE)
                dve.wait_ge(made[WT], r.b + BASE)
                dve.tensor_scalar(w[:, r.side, :, 0:E1], gb[:, :, :], 0.5, None, ALU.mult).then_inc(w_ready, 1)

            def silu(r, x):
                dve.wait_ge(p_ready, 8 * r.b + x + 1 + BASE)
                dve.wait_ge(down_made, 8 * r.b + x - 1 + BASE)
                dve.scalar_tensor_tensor(h2[:, x % 2], ps_g[x % 2][:, :], gate_b[:, x:x + 1], th[:, x % 2],
                                         ALU.add, ALU.mult).then_inc(h2_ready, 1)

            def gather(r, x):
                if x == NS - 1:
                    dve.wait_ge(z_made, r.b + 1 + BASE)
                    for t in range(GROUP):
                        dve.tensor_tensor(acc[:, r.side, t, :], cur[:, r.side, r.cyc, t, :], ps_d[:, tiles(t)],
                                          ALU.add).then_inc(acc_step, 1)
                    return
                e = x - NS
                dve.wait_ge(down_made, 8 * r.b + x + 1 + BASE)
                dve.wait_ge(w_ready, 3 * r.b + 3 + BASE)
                for t in range(GROUP):
                    dve.wait_ge(acc_step, SUMS * r.b + 4 * e + 1 + t + BASE)
                    dve.scalar_tensor_tensor(acc[:, r.side, t, :], ps_d[:, tiles(t)], w[:, r.side, t, e:e + 1], acc[:, r.side, t, :],
                                             ALU.mult, ALU.add).then_inc(acc_step, 1)

            def rms_norm(r):
                dve.wait_ge(rms_ready, r.b + 1 + BASE)
                for t in range(GROUP):
                    dve.scalar_tensor_tensor(cur[:, r.side, r.cyc + 1, t, :], acc[:, r.side, t, :], rms[:, t:t + 1],
                                             weights("norm_w")[:, r.cyc, :], ALU.mult, ALU.mult).then_inc(cur_ready, 1)

            def feature(r, i):
                job, _, _ = FEATURES[i]
                ps = ps_c[:, :].rearrange("p (h m) -> p h m", m=M)
                dve.wait_ge(c_made, CJ * r.b + job + 1 + BASE)
                dve.tensor_reduce(fmax[:, i % 2, :], ps, AX.X, ALU.max).then_inc(f_own, 1)
                dve.wait_ge(f_own, 4 * r.b + i + 1 + BASE)
                dve.tensor_tensor(feat[:, i].rearrange("p (h m) -> p h m", m=M), ps,
                                  fmax[:, i % 2, :].unsqueeze(2).broadcast_to([P, HEADS, M]), ALU.subtract).then_inc(c_read, 1)

            def values(r):
                dve.wait_ge(made[V], r.b + 1 + BASE)
                for t in range(2):
                    ins = dve.tensor_tensor(v[:, r.side, t, :, 0:2 * HD + 2].rearrange("p c (a r) -> p c a r", a=2)[:, :, :, 0:HD],
                                            ps_m[:, tiles(t)].rearrange("p (c a r) -> p c a r", c=C, a=2),
                                            field(core, "vb").rearrange("p (c a r) -> p c a r", c=C, a=2), ALU.add)
                    ins.then_inc(v_ready if t == 0 else read[V], 1)

            def kv_mask(r):
                dve.wait_ge(made[KV], r.b + 1 + BASE)
                dve.tensor_tensor(kv[:, :, :].rearrange("p c r -> p (c r)"), ps_n[:, 0:256], field(core, "kv_mask"),
                                  ALU.mult).then_inc(read[KV], 1)

            def normalise(r):
                ps = ps_m[:, :].rearrange("p (t c r) -> p t c r", t=2, c=C)
                own = Chain(dve, o_own, 4 * r.b)
                dve.wait_ge(made[O], r.b + 1 + BASE)
                for t in range(2):
                    dens = ps[:, t, :, 0:18].rearrange("p c (a r) -> p c a r", a=2)[:, :, :, HD]
                    own.step(dve.tensor_scalar(den[:, t, :].rearrange("p (c a) -> p c a", a=2), dens, 64 * EPS, None, ALU.add))
                dve.wait_ge(o_own, 4 * r.b + 2 + BASE)
                own.link(dve.reciprocal(rec[:, :, :], den[:, :, :]))
                for t in range(2):
                    dve.tensor_tensor(at[:, t].rearrange("p (c a r) -> p c a r", c=C, a=2),
                                      ps[:, t, :, 0:18].rearrange("p c (a r) -> p c a r", a=2)[:, :, :, 0:HD],
                                      rec[:, t, :].rearrange("p (c a) -> p c a", a=2).unsqueeze(3).broadcast_to([P, C, 2, HD]),
                                      ALU.mult).then_inc(o_own if t == 0 else read[O], 1)

            def finish(r):
                dve.wait_ge(made[OUT], r.b + 1 + BASE)
                dve.wait_ge(res_ready, r.group + 1 + BASE)
                two = slice(2 * r.cyc, 2 * r.cyc + 2)
                dve.tensor_tensor(res[:, r.side, two, :], ps_n[:, 0:256].rearrange("p (t d) -> p t d", t=2),
                                  res[:, r.side, two, :], ALU.add).then_inc(read[OUT], 1)

            def moments(r):
                for t in range(GROUP):
                    dve.bn_stats(stats[:, t, :], core.x[:, r.group * GROUP + t, :]).then_inc(st_ready, 1)
                dve.wait_ge(st_ready, 4 * r.group + 4 + BASE)
                carry_wait(core, dve)
                for t in range(GROUP):
                    dve.bn_aggr(mv[:, t, :], stats[:, t, :]).then_inc(mv_ready, 1)

            def norm(r):
                dve.wait_ge(rstd_ready, r.group + 1 + BASE)
                for t in range(GROUP):
                    dve.tensor_scalar(cur[:, r.side, 0, t, :], core.x[:, r.group * GROUP + t, :], mv[:, t, 0:1],
                                      rstd[:, t:t + 1], ALU.subtract, ALU.mult).then_inc(xn_ready, 1)

            def head(r):
                moments(r)
                norm(r)
                values(r)
                logits(r)
                router(r)

            def slot(k, prev, run, nxt):
                if k == 7 and nxt:
                    router(nxt)
                if k == 0 and run:
                    routed(run)
                r, x = behind(k, 1, prev, run)
                if r:
                    silu(r, x)
                r, x = behind(k, 2, prev, run)
                if r and x >= NS - 1:
                    gather(r, x)
                if k == 0 and prev:
                    normalise(prev)
                if k == 3 and prev:
                    finish(prev)
                    rms_norm(prev)
                if nxt and nxt.cyc == 0:
                    if k == 1:
                        moments(nxt)
                    if k == 3:
                        norm(nxt)
                if k == 5 and nxt:
                    values(nxt)
                if k == 6:
                    kv_mask(run)
                    if nxt:
                        logits(nxt)
                if run and k in (0, 1, 2, 4):
                    feature(run, {0: 0, 1: 1, 2: 2, 4: 3}[k])

            over_runs(dve, head, slot)

        @block.scalar
        def _(act):
            act.wait_ge(set_pe, 4 + BASE)
            for half, ps in enumerate((ps_m, ps_n)):
                act.activation(feat[:, 0, N * half:N * half + N], ps[:, :], ACT.Copy).then_inc(set_act, 1)
            for i, banks in enumerate(((ps_u, ps_d), ps_g)):
                for half, ps in enumerate(banks):
                    cols = slice(N * half, N * half + N)
                    act.activation(bp_hi[:, i, cols], ps[0:2, :], ACT.Copy, scale=SCALE).then_inc(set_act, 1)
                    act.activation(feat[0:2, 2 + i, cols], ps[0:2, :], ACT.Copy, scale=SCALE).then_inc(set_act, 1)
            act.wait_ge(set_pool, SET_POOL + BASE)
            act.wait_ge(set_dve, SET_DVE + BASE)

            def up(r, x):
                act.wait_ge(up_made, 8 * r.b + x + 1 + BASE)
                act.wait_ge(p_ready, 8 * r.b + x - 3 + BASE)
                act.activation(h[:, x % 4], ps_u[:, :], ACT.Identity, bias=step(x)[1]).then_inc(h_ready, 1)

            def tanh(r, x):
                act.wait_ge(gate_made, 8 * r.b + x + 1 + BASE)
                act.wait_ge(h2_ready, 8 * r.b + x - 1 + BASE)
                act.activation(th[:, x % 2], ps_g[x % 2][:, :], ACT.Tanh, bias=half_b[:, x:x + 1],
                               scale=0.5).then_inc(th_own, 1)
                act.wait_ge(th_own, 8 * r.b + x + 1 + BASE)
                act.activation(th[:, x % 2], th[:, x % 2], ACT.Copy, bias=1.0).then_inc(th_ready, 1)

            def exp(r, i):
                job, kq, t = FEATURES[i]
                act.wait_ge(c_read, CJ * r.b + job + 1 + BASE)
                act.activation(feat[:, i], feat[:, i], ACT.Exp).then_inc(exped, 1)
                if kq == 0:
                    act.wait_ge(exped, 4 * r.b + i + 1 + BASE)
                    act.activation(feat[:, i], feat[:, i], ACT.Copy, bias=8 * EPS).then_inc(k_ready, 1)

            def q_turned(r, t):
                job = TQ1 if t else TQ0
                act.wait_ge(c_made, CJ * r.b + job + 1 + BASE)
                act.wait_ge(made[OT], r.b + BASE)
                act.activation(qpt[:, :, t, :], ps_c[:, :].rearrange("p (c n) -> p c n", c=C), ACT.Copy,
                               bias=8 * EPS).then_inc(c_read, 1)

            def move(r, job, out, ps):
                act.wait_ge(made[job], r.b + 1 + BASE)
                act.activation(out, ps, ACT.Copy).then_inc(read[job], 1)

            def turn(r):
                move(r, TURN, curt[:, r.side, r.cyc], ps_m[:, :])

            def head(r):
                turn(r)
                top_tanh(r)

            def top_tanh(r):
                act.wait_ge(tanh_in, r.b + 1 + BASE)
                act.activation(top[:, :], top[:, :], ACT.Tanh, scale=0.5).then_inc(tanh_out, 1)

            def slot(k, prev, run, nxt):
                if run:
                    tanh(run, k)
                    up(run, k)
                if k == 1 and prev:
                    move(prev, AT, att[:, :, :].rearrange("p t n -> p (t n)"), ps_n[:, 0:256])
                if run:
                    if k == 1:
                        move(run, WT, wt[:, :], ps_m[0:8, :])
                    if k == 5:
                        move(run, KVT, kvt[:, :, :].rearrange("p a n -> p (a n)"), ps_n[:, 0:256])
                    if k == 7:
                        move(run, OT, ot[:, :, :, :].rearrange("p a t n -> p (a t n)"), ps_n[:, :])
                    if k in (1, 2, 3, 5):
                        exp(run, {1: 0, 2: 1, 3: 2, 5: 3}[k])
                    if k in (3, 6):
                        q_turned(run, k // 6)
                if k == 4 and nxt:
                    turn(nxt)
                if k == 7 and nxt:
                    top_tanh(nxt)
                if k == 2 and prev:
                    act.wait_ge(acc_step, SUMS * prev.b + SUMS + BASE)
                    for t in range(GROUP):
                        act.wait_ge(msq_ready, 4 * prev.b + t + BASE)
                        act.activation(sq[:, :], acc[:, prev.side, t, :], ACT.Square, accum_out=msq[:, t:t + 1]).then_inc(msq_ready, 1)

            over_runs(act, head, slot)

        @block.tensor
        def _(pe):
            def composite(name):
                for j in range(2):
                    last = pe.matmul(ps_c[:, N * j:N * j + N], field(core, name), field(core, "proj")[:, N * j:N * j + N],
                                     start=True, stop=True)
                last.then_inc(set_pe, 1)

            composite("kw")
            for i, banks in enumerate(((ps_u, ps_d), ps_g)):
                for j, ps in enumerate(banks):
                    last = pe.matmul(ps[0:2, :], field(core, "qkb")[:, 2 * i:2 * i + 2],
                                     field(core, "proj")[:, N * j:N * j + N], start=True, stop=True)
                last.then_inc(set_pe, 1)
            for x in range(STEPS):
                last = pe.transpose((ps_m, ps_n)[x // 4][:, tiles(x % 4)], step(x)[0], ident)
            last.then_inc(set_pe, 1)
            pe.wait_ge(set_dve, 2 + BASE)
            composite("qw")
            pe.wait_ge(set_act, 4 + 2 + BASE)
            for x in range(STEPS):
                pe.matmul((ps_m, ps_n)[x // 4][:, tiles(x % 4)], feat[:, 0, tiles(x)], step(x)[2], start=True, stop=True)
            for x in range(STEPS):
                last = pe.matmul(ps_u[:, x:x + 1], step(x)[2], step(x)[1], start=True, stop=True)
            last.then_inc(set_pe, 1)
            pe.wait_ge(set_dve, SET_DVE + BASE)
            pe.wait_ge(set_pool, SET_POOL + BASE)

            def after(job, count):
                pe.wait_ge(read[job], count + BASE)

            def turn(r):
                if r.cyc == 0:
                    pe.wait_ge(xn_ready, 4 * r.group + 4 + BASE)
                else:
                    pe.wait_ge(cur_ready, 4 * r.b - 4 + BASE)
                for t in range(GROUP):
                    last = pe.transpose(ps_m[:, tiles(t)], cur[:, r.side, r.cyc, t, :], ident)
                last.then_inc(made[TURN], 1)

            def logits(r):
                for t in range(GROUP):
                    last = pe.matmul(ps_m[:, t * E1:(t + 1) * E1], curt[:, r.side, r.cyc, tiles(t)],
                                     field(core, "router")[:, r.cyc * E1:(r.cyc + 1) * E1], start=True, stop=True)
                last.then_inc(made[GATE], 1)

            def tokens(r, t):
                return [a[:, r.side, 0, tiles(2 * r.cyc + t)] for a in (curt, x_hi, x_lo)]

            def comb(r, i):
                job, kq, t = FEATURES[i]
                pe.wait_ge(c_read, CJ * r.b + job + BASE)
                for j in range(2):
                    cols = slice(512 * j, 512 * j + 512)
                    product(pe, ps_c[:, cols], tokens(r, t)[1:], (wp_hi[:, kq, cols], wp_lo[:, kq, cols]), stop=False)
                    last = pe.matmul(ps_c[:, cols], ones[:, :], bp[:, kq, cols], start=False, stop=True)
                last.then_inc(c_made, 1)

            def turn_q(r, t):
                job = TQ1 if t else TQ0
                pe.wait_ge(c_read, CJ * r.b + job + BASE)
                pe.wait_ge(exped, 4 * r.b + 2 + 2 * t + BASE)
                for c in range(C):
                    last = pe.transpose(ps_c[:, tiles(c)], feat[:, 2 * t + 1, tiles(c)], ident)
                last.then_inc(c_made, 1)

            def values(r):
                for t in range(2):
                    last = pe.matmul(ps_m[:, tiles(t)], tokens(r, t)[0], field(core, "vw"), start=True, stop=True)
                last.then_inc(made[V], 1)

            def turn_weights(r):
                pe.wait_ge(w_ready, 3 * r.b + 3 + BASE)
                for t in range(GROUP):
                    last = pe.transpose(ps_m[0:8, tiles(t)], w[:, r.side, t, :], ident)
                last.then_inc(made[WT], 1)

            def key_values(r):
                pe.wait_ge(k_ready, 2 * r.b + 2 + BASE)
                for a in range(2):
                    for t in range(2):
                        for j in range(4):
                            c = 4 * a + j
                            last = pe.matmul(ps_n[32 * j:32 * j + 32, tiles(a)], v[:, r.side, t, c, :],
                                             feat[:, 2 * t, tiles(c)], start=t == 0, stop=t == 1)
                last.then_inc(made[KVT], 1)

            def turn_key_values(r):
                for a in range(2):
                    last = pe.transpose(ps_n[:, tiles(a)], kvt[:, a, :], ident)
                last.then_inc(made[KV], 1)

            def attend(r):
                pe.wait_ge(c_read, CJ * r.b + CJ + BASE)
                for a in range(2):
                    for j in range(4):
                        c = 4 * a + j
                        last = pe.matmul(ps_n[32 * j:32 * j + 32, 256 * a:256 * a + 256], kv[:, c, :],
                                         qpt[:, c, :, :].rearrange("p t n -> p (t n)"), start=True, stop=True)
                last.then_inc(made[OT], 1)

            def turn_attended(r):
                pe.wait_ge(read[OT], r.b + 1 + BASE)
                for t in range(2):
                    for a in range(2):
                        last = pe.transpose(ps_m[:, tiles(2 * t + a)], ot[:, a, t, :], ident)
                last.then_inc(made[O], 1)

            def turn_output(r):
                for t in range(2):
                    last = pe.transpose(ps_n[:, tiles(t)], at[:, t, :], ident)
                last.then_inc(made[AT], 1)

            def project(r):
                for t in range(2):
                    last = pe.matmul(ps_n[:, tiles(t)], att[:, t, :], field(core, "pw"), start=True, stop=True)
                last.then_inc(made[OUT], 1)

            def gate(r, x):
                pe.wait_ge(h2_ready, 8 * r.b + x - 1 + BASE)
                if x == 0:
                    pe.wait_ge(lo_ready, r.b + 1 + BASE)
                product(pe, ps_g[x % 2][:, :], (gate_hi[:, x, :], gate_lo[:, x, :]),
                        (x_hi[:, r.side, r.cyc], x_lo[:, r.side, r.cyc])).then_inc(gate_made, 1)

            def up(r, x):
                pe.wait_ge(h_ready, 8 * r.b + x + BASE)
                product(pe, ps_u[:, :], (up_hi[:, x, :], up_lo[:, x, :]),
                        (x_hi[:, r.side, r.cyc], x_lo[:, r.side, r.cyc])).then_inc(up_made, 1)

            def down_step(r, x):
                pe.wait_ge(h2_ready, 8 * r.b + x + 1 + BASE)
                pe.wait_ge(acc_step, SUMS * r.b + (4 * (x - NS) + 4 if x >= NS else 0) + BASE)
                for t in range(GROUP):
                    last = pe.matmul(ps_d[:, tiles(t)], h2[:, x % 2, tiles(t)],
                                     down[:, step(x)[4], :], start=(x == 0 and t == 0) or x >= NS, stop=x >= NS,
                                     skip_group_check=True)
                last.then_inc(down_made, 1)

            def biases(r):
                pe.wait_ge(read[WT], r.b + 1 + BASE)
                for t in range(GROUP):
                    last = pe.matmul(ps_d[:, tiles(t)], wt[:, tiles(t)], field(core, "down_b")[0:8, :], start=False,
                                     stop=t == GROUP - 1, skip_group_check=True)
                last.then_inc(z_made, 1)

            def head(r):
                turn(r)
                after(TURN, r.b + 1)
                values(r)
                after(V, r.b + 1)
                logits(r)

            def slot(k, prev, run, nxt):
                if run:
                    gate(run, k)
                r, x = behind(k, 2, prev, run)
                if r:
                    down_step(r, x)
                    if x == NS - 1:
                        biases(r)
                if run:
                    up(run, k)
                if k == 0 and prev:
                    after(GATE, prev.b + 2) if run else after(WT, prev.b + 1)
                    after(OT, prev.b + 1)
                    turn_attended(prev)
                if k == 1:
                    if prev:
                        after(O, prev.b + 1)
                        turn_output(prev)
                    else:
                        after(GATE, run.b + 1)
                    if run:
                        turn_weights(run)
                if k == 2 and prev:
                    after(AT, prev.b + 1)
                    project(prev)
                if k == 4 and nxt:
                    after(WT, run.b + 1)
                    turn(nxt)
                if k == 5:
                    after(OUT, run.b)
                    key_values(run)
                    if nxt:
                        after(TURN, nxt.b + 1)
                        values(nxt)
                if k == 6:
                    after(KVT, run.b + 1)
                    turn_key_values(run)
                    if nxt:
                        after(V, nxt.b + 1)
                        logits(nxt)
                if k == 7:
                    after(KV, run.b + 1)
                    attend(run)
                if run and k in (0, 1, 2, 4):
                    comb(run, {0: 0, 1: 1, 2: 2, 4: 3}[k])
                if run and k in (3, 6):
                    turn_q(run, k // 6)

            over_runs(pe, head, slot)


def build(nc, x, pack, out, debug=None, stop=None):
    core = Core()
    with ExitStack() as ctx:
        sb = lambda name, shape, dt=F32: ctx.enter_context(nc.sbuf_tensor(name, shape, dt))
        core.passed = ctx.enter_context(nc.semaphore("passed"))
        core.x = sb("x", [P, TILES, P])
        core.pack = sb("pack", [P, PACK])
        core.minus_half = sb("minus_half", [P, 16])
        with ExitStack() as ctx0:
            sb = lambda name, shape, dt=F32: ctx0.enter_context(nc.sbuf_tensor(name, shape, dt))
            core.pack_0 = sb("pack_0", [P, PACK_0])
            core.xnt = sb("xnt", [P, TILES * P])
            core.mean = sb("mean", [P, TILES])
            core.rstd = sb("rstd", [P, TILES])
            core.probs = sb("probs", [P, TILES, E0])
            core.gates = sb("gates", [P, TILES, E0])
            norm_block(nc, core, x, pack)
            choice_block(nc, core)
            attention_block(nc, core)
            if debug and stop == 3:
                debug(nc, core, out)
                return
            expert_block(nc, core)
            if debug and stop == 4:
                debug(nc, core, out)
                return
        second_block(nc, core, out)


def _pack(v):
    import numpy as np

    f = np.float32
    put = {}
    p = np.arange(P)
    put["ident"] = np.eye(P, dtype=f)
    put["same_expert"] = (p[:, None] % E0 == p[None, :] % E0).astype(f)
    put["before"] = (p[:, None] < p[None, :]).astype(f)
    put["ones"] = np.ones((P, P), f)
    put["rev_expert"] = np.broadcast_to((E0 - np.arange(E0)).astype(f), (P, E0))
    put["positions"] = np.broadcast_to(np.arange(SEQ, dtype=f), (P, SEQ))
    put["inv_base"] = (10000.0 ** (-2.0 * (p - p % 2) / P)).astype(f)[:, None]
    put["phase"] = np.where(p % 2 == 1, np.pi / 2, 0.0).astype(f)[:, None]
    put["lo_q"] = -((p % 32 // 8) == 2).astype(f)[:, None]
    put["lo_k"] = -((p % 32 // 8) == 1).astype(f)[:, None]
    put["ones_k"] = ((p % 32 == 24) | (p % 32 == 25)).astype(f)[:, None]
    put["bias_lo"] = -(p == 1).astype(f)[:, None]
    cc = np.arange(256) % 32
    put["kv_mask"] = ((cc[None, :] // 9 == p[:, None] // 64) & (cc[None, :] < 18)).astype(f)
    wide = lambda a: np.broadcast_to(np.asarray(a).reshape(1, -1), (P, np.asarray(a).size))
    put["rby"] = wide(v["L0_attn_rby"])

    def stacked(a):
        a = a.reshape(a.shape[0], 4, 4, HD)
        return np.concatenate([a, a, a, np.zeros_like(a)], axis=-1).reshape(a.shape[0], 512)

    put["wq"] = stacked(v["L0_attn_Wq"].T)
    put["wk"] = stacked(v["L0_attn_Wk"].T)
    put["bq"] = stacked(v["L0_attn_bq"][None, :]).reshape(4, P).T
    put["bk"] = stacked(v["L0_attn_bk"][None, :]).reshape(4, P).T
    put["wv"], put["wo"] = v["L0_attn_Wv"].T, v["L0_attn_Wo"].T
    put["bv"], put["bo"] = wide(v["L0_attn_bv"]), wide(v["L0_attn_bo"])
    put["gamma"], put["beta"] = wide(v["L0_attn_ln_gamma"]), wide(v["L0_attn_ln_beta"])
    put["wg"] = v["L0_ffn_Wg"]
    put["w1"] = v["L0_ffn_W1"].transpose(1, 0, 2).reshape(P, E0 * F0)
    put["w2"] = v["L0_ffn_W2"].reshape(E0, 2, P, P).transpose(2, 0, 1, 3).reshape(P, E0 * 2 * P)
    w = v["L1_attn_qkv_w"]
    put["qw"], put["kw"], put["vw"] = w[0:P], w[P:2 * P], w[2 * P:3 * P].T
    b = v["L1_attn_qkv_b"]
    put["qkb"] = np.stack([b[P:2 * P], b[P:2 * P], b[0:P], b[0:P]], axis=1)
    put["vb"] = wide(b[2 * P:3 * P])
    pm = np.asarray(v["L1_attn_projection_matrix"])
    proj = np.zeros((HEADS, HD, HEADS, M), f)
    for h in range(HEADS):
        proj[h, :, h, :] = pm.T
    put["proj"] = proj.reshape(P, HEADS * M)
    put["pw"], put["pb"] = v["L1_attn_proj_w"].T, wide(v["L1_attn_proj_b"])
    put["router"] = v["L1_ffn_router_W"].transpose(1, 0, 2).reshape(P, CYCLES * E1)
    put["router_b"], put["gate_b"] = wide(v["L1_ffn_router_b"]), wide(v["L1_ffn_gate_bias"])
    put["up"] = v["L1_ffn_exp_Wup"].transpose(1, 0, 2).reshape(P, E1 * P)
    put["gw"] = v["L1_ffn_exp_Wg"].transpose(1, 0, 2).reshape(P, E1 * P)
    put["down"] = v["L1_ffn_exp_Wdown"].transpose(1, 0, 2).reshape(P, E1 * P)
    put["up_b"], put["gw_b"] = v["L1_ffn_exp_bup"].T, v["L1_ffn_exp_bg"].T
    db = np.zeros((P, P), f)
    db[0:E1], db[E1] = v["L1_ffn_exp_bdown"], v["L1_ffn_share_bdown"]
    put["down_b"] = db
    put["s_up"], put["s_up_b"] = v["L1_ffn_share_Wup"], v["L1_ffn_share_bup"].reshape(NS, P).T
    put["s_gw"], put["s_gw_b"] = v["L1_ffn_share_Wg"], v["L1_ffn_share_bg"][:, None]
    put["s_down"] = v["L1_ffn_share_Wdown"]
    put["norm_w"] = wide(v["L1_ffn_norm_w"])
    return np.ascontiguousarray(np.concatenate([np.asarray(put[name]).reshape(P, width) for name, width in FIELDS + FIELDS_0], axis=1))


def kernel(**inputs):
    import numpy as np
    import concourse.bacc as bacc
    from concourse.bass_utils import run_bass_kernel_spmd

    nc = bacc.Bacc("TRN2", target_bir_lowering=False, num_devices=1)
    v = {k: np.asarray(a) for k, a in inputs.items()}
    arrays = {
        "x_dram": np.ascontiguousarray(v["L0_attn_x"].reshape(TILES * P, P)),
        "pack_dram": _pack(v),
    }
    x = nc.dram_tensor("x_dram", (TILES * P, P), F32, kind="ExternalInput").ap()
    pack = nc.dram_tensor("pack_dram", (P, PACK + PACK_0), F32, kind="ExternalInput").ap()
    out = nc.dram_tensor("out_dram", (TILES * P, P), F32, kind="ExternalOutput").ap()
    build(nc, x, pack, out)
    r = run_bass_kernel_spmd(nc, [arrays], core_ids=[0])
    return r.results[0]["out_dram"].reshape(BATCH, SEQ, P)
```
